# Optimizing a Trainium2 kernel written in Bass

```python
import numpy as np
import jax
import jax.numpy as jnp

def _softmax(x, axis=-1):
    return jax.nn.softmax(x, axis=axis)

def _gelu(x):
    return jax.nn.gelu(x, approximate=True)

def _silu(x):
    return jax.nn.silu(x)

def _sigmoid(x):
    return jax.nn.sigmoid(x)

def _layernorm(x, axis=-1, eps=1e-05):
    m = jnp.mean(x, axis=axis, keepdims=True)
    v = jnp.var(x, axis=axis, keepdims=True)
    return (x - m) / jnp.sqrt(v + eps)

def _scatter_add(tgt, idx, src, axis=0):
    return tgt.at[idx].add(src)

def _segment_sum(src, seg, n):
    return jax.ops.segment_sum(src, seg, n)
kernel_name = 'mk_gnn_resnorm_d2_gnn_r32_b7b5a7'

def setup_inputs(seed: int=0):
    np.random.seed(seed)
    _w = jnp.asarray

    def _rec_inputs():
        import jax
        import jax.numpy as jnp
        _gk = jax.random.key(seed)
        x = -0.0003713 + 1 * jax.random.normal(jax.random.fold_in(_gk, 1), (3125, 256), jnp.float32)
        src = jax.random.randint(jax.random.fold_in(_gk, 2), (50000,), 0, 3125, jnp.int32)
        dst = jax.random.randint(jax.random.fold_in(_gk, 3), (50000,), 0, 3125, jnp.int32)
        _o = jnp.argsort(dst, stable=True)
        src = src[_o]
        dst = dst[_o]
        edge_type_16 = jax.random.randint(jax.random.fold_in(_gk, 13), (50000,), 0, 16, jnp.int32)
        return (x, src, dst, edge_type_16)
    x, src, dst, edge_type_16 = _rec_inputs()

    def _L0_gnn_setup():
        import jax, jax.numpy as jnp
        import numpy as np
        N, E = (50000, 25000)
        IN_DIM, HEADS, OUT_DIM = (256, 8, 32)
        NEG_SLOPE = 0.2
        LN_EPS = 1e-05
        key = jax.random.key(seed)
        ks = jax.random.split(key, 8)
        HC = HEADS * OUT_DIM
        x = jax.random.normal(ks[0], (N, IN_DIM), dtype=jnp.float32)
        edge_index = jax.random.randint(ks[1], (2, E), 0, N, dtype=jnp.int32)
        W = jax.random.normal(ks[2], (IN_DIM, HC), dtype=jnp.float32) / np.sqrt(IN_DIM)
        att_src = jax.random.normal(ks[3], (HEADS, OUT_DIM), dtype=jnp.float32) / np.sqrt(OUT_DIM)
        att_dst = jax.random.normal(ks[4], (HEADS, OUT_DIM), dtype=jnp.float32) / np.sqrt(OUT_DIM)
        bias = jnp.zeros((HC,), dtype=jnp.float32)
        ln_gamma = jnp.ones((HC,), dtype=jnp.float32)
        ln_beta = jnp.zeros((HC,), dtype=jnp.float32)
        return {'x': x, 'edge_index': edge_index, 'W': W, 'att_src': att_src, 'att_dst': att_dst, 'bias': bias, 'ln_gamma': ln_gamma, 'ln_beta': ln_beta}
    _L0_gnn_all = _L0_gnn_setup()
    _L0_gnn_in = {k: v for k, v in _L0_gnn_all.items() if k in ('W', 'att_src', 'att_dst', 'bias', 'ln_gamma', 'ln_beta')}
    del _L0_gnn_all

    def _L1_gnn_setup():
        import jax, jax.numpy as jnp
        import numpy as np
        from jax.ops import segment_sum
        N_NODES = 10000
        N_EDGES = 5000
        IN_FEAT = 256
        OUT_FEAT = 256
        NUM_RELS = 16

        def _inv_degree(idx, n):
            deg = segment_sum(jnp.ones(idx.shape[0], dtype=jnp.float32), idx, num_segments=n)
            return jnp.where(deg > 0, 1.0 / deg, 0.0)

        def _typed_pass(feat, W, bias, src_idx, dst_idx, etypes, norm_per_edge, n):
            proj = jnp.einsum('ni,rio->rno', feat, W)
            m = proj[etypes, src_idx] + bias
            m = m * norm_per_edge[:, None]
            return segment_sum(m, dst_idx, num_segments=n)
        key = jax.random.key(seed)
        ks = jax.random.split(key, 8)
        feat = jax.random.normal(ks[0], (N_NODES, IN_FEAT), dtype=jnp.float32)
        Wf = jax.random.normal(ks[1], (NUM_RELS, IN_FEAT, OUT_FEAT), dtype=jnp.float32)
        Wb = jax.random.normal(ks[2], (NUM_RELS, IN_FEAT, OUT_FEAT), dtype=jnp.float32)
        loop_weight = jax.random.normal(ks[3], (IN_FEAT, OUT_FEAT), dtype=jnp.float32)
        forward_bias = jnp.zeros((OUT_FEAT,), dtype=jnp.float32)
        backward_bias = jnp.zeros((OUT_FEAT,), dtype=jnp.float32)
        self_bias = jnp.zeros((OUT_FEAT,), dtype=jnp.float32)
        src = jax.random.randint(ks[4], (N_EDGES,), 0, N_NODES, dtype=jnp.int32)
        dst = jax.random.randint(ks[5], (N_EDGES,), 0, N_NODES, dtype=jnp.int32)
        etypes = jax.random.randint(ks[6], (N_EDGES,), 0, NUM_RELS, dtype=jnp.int32)
        return {'feat': feat, 'Wf': Wf, 'Wb': Wb, 'loop_weight': loop_weight, 'forward_bias': forward_bias, 'backward_bias': backward_bias, 'self_bias': self_bias, 'src': src, 'dst': dst, 'etypes': etypes, 'use_dis_weight': 0, 'drop_out': 0}
    _L1_gnn_all = _L1_gnn_setup()
    _L1_gnn_in = {k: v for k, v in _L1_gnn_all.items() if k in ('Wf', 'Wb', 'loop_weight', 'forward_bias', 'backward_bias', 'self_bias')}
    del _L1_gnn_all
    return {'x': x, 'src': src, 'dst': dst, 'edge_type_16': edge_type_16, 'L0_gnn_W': _L0_gnn_in['W'], 'L0_gnn_att_src': _L0_gnn_in['att_src'], 'L0_gnn_att_dst': _L0_gnn_in['att_dst'], 'L0_gnn_bias': _L0_gnn_in['bias'], 'L0_gnn_ln_gamma': _L0_gnn_in['ln_gamma'], 'L0_gnn_ln_beta': _L0_gnn_in['ln_beta'], 'L1_gnn_Wf': _L1_gnn_in['Wf'], 'L1_gnn_Wb': _L1_gnn_in['Wb'], 'L1_gnn_loop_weight': _L1_gnn_in['loop_weight'], 'L1_gnn_forward_bias': _L1_gnn_in['forward_bias'], 'L1_gnn_backward_bias': _L1_gnn_in['backward_bias'], 'L1_gnn_self_bias': _L1_gnn_in['self_bias']}

def reference(x, src, dst, edge_type_16, L0_gnn_W, L0_gnn_att_src, L0_gnn_att_dst, L0_gnn_bias, L0_gnn_ln_gamma, L0_gnn_ln_beta, L1_gnn_Wf, L1_gnn_Wb, L1_gnn_loop_weight, L1_gnn_forward_bias, L1_gnn_backward_bias, L1_gnn_self_bias):
    import jax
    import jax.numpy as jnp

    def _L0_gnn_ref(x, edge_index, W, att_src, att_dst, bias, ln_gamma, ln_beta):
        import jax, jax.numpy as jnp
        import numpy as np
        N, E = (50000, 25000)
        IN_DIM, HEADS, OUT_DIM = (256, 8, 32)
        NEG_SLOPE = 0.2
        LN_EPS = 1e-05
        n = x.shape[0]
        loop = jnp.arange(n, dtype=edge_index.dtype)
        src = jnp.concatenate([edge_index[0], loop])
        dst = jnp.concatenate([edge_index[1], loop])
        h = (x @ W).reshape(n, HEADS, OUT_DIM)
        a_src = jnp.einsum('nhc,hc->nh', h, att_src)
        a_dst = jnp.einsum('nhc,hc->nh', h, att_dst)
        e = jax.nn.leaky_relu(a_src[src] + a_dst[dst], NEG_SLOPE)
        m = jax.ops.segment_max(e, dst, num_segments=n)
        e = jnp.exp(e - m[dst])
        denom = jax.ops.segment_sum(e, dst, num_segments=n)
        alpha = e / (denom[dst] + 1e-16)
        out = jax.ops.segment_sum(h[src] * alpha[:, :, None], dst, num_segments=n)
        out = out.reshape(n, HEADS * OUT_DIM) + bias
        mu = jnp.mean(out, axis=-1, keepdims=True)
        var = jnp.mean(jnp.square(out - mu), axis=-1, keepdims=True)
        return ln_gamma * (out - mu) * jax.lax.rsqrt(var + LN_EPS) + ln_beta

    def _L1_gnn_ref(feat, Wf, Wb, loop_weight, forward_bias, backward_bias, self_bias, src, dst, etypes, use_dis_weight, drop_out):
        import jax, jax.numpy as jnp
        import numpy as np
        from jax.ops import segment_sum
        N_NODES = 10000
        N_EDGES = 5000
        IN_FEAT = 256
        OUT_FEAT = 256
        NUM_RELS = 16

        def _inv_degree(idx, n):
            deg = segment_sum(jnp.ones(idx.shape[0], dtype=jnp.float32), idx, num_segments=n)
            return jnp.where(deg > 0, 1.0 / deg, 0.0)

        def _typed_pass(feat, W, bias, src_idx, dst_idx, etypes, norm_per_edge, n):
            proj = jnp.einsum('ni,rio->rno', feat, W)
            m = proj[etypes, src_idx] + bias
            m = m * norm_per_edge[:, None]
            return segment_sum(m, dst_idx, num_segments=n)
        n = feat.shape[0]
        norm_f = _inv_degree(dst, n)[dst]
        m_forward = _typed_pass(feat, Wf, forward_bias, src, dst, etypes, norm_f, n)
        norm_b = _inv_degree(src, n)[src]
        m_backward = _typed_pass(feat, Wb, backward_bias, dst, src, etypes, norm_b, n)
        s = feat @ loop_weight
        s = s + s + self_bias
        return s + m_forward + m_backward
    edge_index = jnp.stack([src, dst])
    x = _layernorm(x + _L0_gnn_ref(x, edge_index, L0_gnn_W, L0_gnn_att_src, L0_gnn_att_dst, L0_gnn_bias, L0_gnn_ln_gamma, L0_gnn_ln_beta), axis=-1)
    x = _layernorm(x + _L1_gnn_ref(x, L1_gnn_Wf, L1_gnn_Wb, L1_gnn_loop_weight, L1_gnn_forward_bias, L1_gnn_backward_bias, L1_gnn_self_bias, src, dst, edge_type_16, 0, 0), axis=-1)
    return x

_drawn_inputs = setup_inputs


def setup_inputs(seed=0):
    import zlib

    import numpy as np

    out = dict(_drawn_inputs(seed))
    spreads = {'L0_gnn_bias': (0.0, 0.1),
     'L0_gnn_ln_gamma': (1.0, 0.2),
     'L0_gnn_ln_beta': (0.0, 0.1),
     'L1_gnn_forward_bias': (0.0, 2.0),
     'L1_gnn_backward_bias': (0.0, 2.0),
     'L1_gnn_self_bias': (0.0, 2.0)}
    factors = {}
    for name, (base, spread) in spreads.items():
        noise = np.random.default_rng([zlib.crc32(name.encode()), seed]).standard_normal(out[name].shape)
        drawn = base * np.exp(spread * noise) if base else spread * noise
        out[name] = jnp.asarray(drawn.astype(out[name].dtype))
    for name, factor in factors.items():
        out[name] = (out[name] * factor).astype(out[name].dtype)
    return out
```

```python
import numpy as np
import concourse.bass as bass
from concourse import mybir
from contextlib import ExitStack

P = 128
N, D, H, R = 3125, 256, 8, 16
HC = D // H
E = 50000
NL = 125
NT = N // NL
C0 = 392
FULL = E // C0
REST = E - FULL * C0
T1 = 416
T2 = 792
assert T1 * P >= E + (P - 1) * NT and T2 * P >= E + (P - 1) * NT * R
HW = D + H
XW = D + 2 * H
G = 4
OFF = 1600
FAR = 128.0 * 1024
ABSENT = -(2.0 ** 100)
LN_EPS = 1e-5

f32, f16, bf16 = mybir.dt.float32, mybir.dt.float16, mybir.dt.bfloat16
i16, i32 = mybir.dt.int16, mybir.dt.int32
ALU = mybir.AluOpType
ACT = mybir.ActivationFunctionType
AX = mybir.AxisListType
ds = bass.ds


class Steps:

    def __init__(self, sem):
        self.sem, self.base, self.k, self.i, self.per = sem, 0, 0, None, 0

    def loop(self, i, per):
        self.i, self.per, self.k = i, per, 0

    def end(self, times):
        assert self.k == self.per, (self.k, self.per)
        self.base += self.per * times
        self.i, self.k = None, 0

    @property
    def now(self):
        if self.i is None:
            return self.base
        return self.base + self.i * self.per + self.k

    def step(self):
        if self.i is None:
            self.base += 1
        else:
            self.k += 1
        return self.now


def build_program(nc, a, out):
    ctx = ExitStack()
    with ctx:
        def sb(name, shape, dt=f32):
            return ctx.enter_context(nc.sbuf_tensor(name, shape, dt))

        def sem(name):
            return ctx.enter_context(nc.semaphore(name))

        h_table = nc.dram_tensor("h_table", (N, HW), f32).ap()
        s_table = nc.dram_tensor("s_table", (N, 3 * H), bf16).ap()
        x_table = nc.dram_tensor("x_table", (N, D), f32).ap()

        X = sb("X", [NL, NT, D])
        ACC = [sb(f"ACC{d}", [NL, NT, XW]) for d in (0, 1)]
        Hn = ACC[1]
        WR = sb("WR", [P, 2 * R * 2 * D])
        bc = sb("bc", [P, 8, D])
        Wg = sb("Wg", [P, 2, XW])
        Wl = sb("Wl", [P, 2, D])
        identf = sb("identf", [P, P])
        identb = sb("identb", [P, P], bf16)
        trif = sb("trif", [P, P])
        triif = sb("triif", [P, P])
        tri16 = sb("tri16", [P, P], f16)
        ones16 = sb("ones16", [P, P], f16)
        onesf = sb("onesf", [P, P])
        zero16 = sb("zero16", [P, P], f16)
        sel = sb("sel", [3 * H, H, P], bf16)
        nbig = sb("nbig", [P, G, P], bf16)
        iota16 = sb("iota16", [P, T2], f16)
        iotaf = sb("iotaf", [P, P])
        pidx_i = sb("pidx_i", [P, 1], i32)
        pidx = sb("pidx", [P, 1])
        idx1 = sb("idx1", [P, T1 + 2 * G], i16)
        lo1 = sb("lo1", [P, T1])
        tile1 = sb("tile1", [P, T1], i32)
        idx2 = [sb(f"idx2{d}", [P, T2 + 2 * G], i16) for d in (0, 1)]
        lo2 = [sb(f"lo2{d}", [P, T2]) for d in (0, 1)]
        maps = sb("maps", [P, T2], i32)
        tile2 = [maps[64 * d:64 * d + 1, :] for d in (0, 1)]
        rel2 = [maps[64 * d + 32:64 * d + 33, :] for d in (0, 1)]
        M = sb("M", [NL, NT, H])
        ADC = sb("ADC", [NL, NT, 2 * H])
        ring = sb("ring", [P, 8, HW])
        row = ring[0:1, :, 0:D]
        idxc = sb("idxc", [P, 8], i32)
        oh = sb("oh", [P, 8, NL])
        scaled = sb("scaled", [P, 4, HW])
        ohT = sb("ohT", [NL, 4, P])
        small = sb("small", [P, 4, G * H])
        noh = sb("noh", [P, 4, NL], bf16)
        sring = sb("sring", [P, 8, 3 * H], bf16)
        asT = sb("asT", [3 * H, 2, P], bf16)
        mx = sb("mx", [NL, H])
        stab = sb("stab", [NL, NT, 3 * H], bf16)
        n0, n1, n2 = (sb(f"n{k}", [NL, NT, H]) for k in range(3))
        stat = sb("stat", [NL, NT, 4])
        att = scaled
        xs = sb("xs", [NL, D])
        PS = ctx.enter_context(nc.psum_tensor("PS", [P, 8, 512], f32))

        at = [0]

        def cut(words):
            at[0] += words
            assert at[0] <= 2 * R * 2 * D
            return WR[:, at[0] - words:at[0]]

        own_i, oth_i, typ_i = (cut(C0).bitcast(i32) for _ in range(3))
        hi, lo, Av, Bv, t0, t1, t2, pos, jf, sf = (cut(T1) for _ in range(10))
        rowtot, offs, r0, r1 = (cut(NT) for _ in range(4))
        c0, c1, c2, c3 = (cut(1) for _ in range(4))
        cmp16 = cut(T2 // 2).bitcast(f16)
        dmap = cut(T1)
        A1, B1, typ1 = (cut(T1) for _ in range(3))
        masks = cut(R * T1 // 2).bitcast(f16).rearrange("p (t j) -> p t j", t=R)
        cntj = cut(4 * R)
        dT = cut(4 * NT)
        cnt, end2, shift, s0, s1 = (cut(R) for _ in range(5))
        shiftb = cut(P)
        ohj = cut(4 * (T2 // 2)).bitcast(f16).rearrange("p (u j) -> p u j", u=4)
        lab = cut(4 * P).bitcast(f16).rearrange("p (u k s) -> p u k s", u=4, k=2)
        q0, q1, q2 = (cut(T2) for _ in range(3))
        iota_i = q2.bitcast(i32)
        onesw = cut(T1)

        gate = sem("gate")
        filled = sem("filled")
        made = sem("made")
        x_in, w_in, rows_in, wr_in = sem("x_in"), sem("w_in"), sem("rows_in"), sem("wr_in")
        edges_in = [sem(f"edges_in{d}") for d in (0, 1)]
        vs = sem("vs")
        spread = sem("spread")
        wg_ready = sem("wg_ready")
        act_lin, pe_lin = sem("act_lin"), sem("pe_lin")
        sort_in, sort_out = sem("sort_in"), sem("sort_out")
        perm_in, perm_out = sem("perm_in"), sem("perm_out")
        sort_done = sem("sort_done")
        tab_ready = sem("tab_ready")
        h_out, s_out, x_out = sem("h_out"), sem("s_out"), sem("x_out")
        gath = [sem(f"gath{u}") for u in range(8)]
        idx_ready, slot_free = sem("idx_ready"), sem("slot_free")
        noh_ready, turned, ast_ready = sem("noh_ready"), sem("turned"), sem("ast_ready")
        v_done, max_taken = sem("v_done"), sem("max_taken")
        oh_ready, oht_ps, oht_ready = sem("oh_ready"), sem("oht_ps"), sem("oht_ready")
        adc_done, z_ready, p_ready = sem("adc_done"), sem("z_ready"), sem("p_ready")
        hp_ready, agg_done, acc_taken = sem("hp_ready"), sem("agg_done"), sem("acc_taken")
        shift_ready, self_exp = sem("shift_ready"), sem("self_exp")
        moh_ready, at_ps, at_ready = sem("moh_ready"), sem("at_ps"), sem("at_ready")
        y_done, y_taken = sem("y_done"), sem("y_taken")
        ln_act, ln_in = sem("ln_act"), sem("ln_in")
        fin_act, fin_ps, fin_taken = sem("fin_act"), sem("fin_ps"), sem("fin_taken")
        out_ready, out_done = sem("out_ready"), sem("out_done")

        block = ctx.enter_context(nc.Block())

        def node_rows(t):
            return t.rearrange("(t p) f -> p t f", p=NL)

        WV = WR[:, :].rearrange("p (d r c o) -> p d r c o", d=2, r=R, c=2)
        dbg = a.get("dbg", {})
        loc = locals()

        @block.sync
        def _(sp):
            for k, name in enumerate(("L0_gnn_att_src", "L0_gnn_att_dst", "L0_gnn_bias", "L0_gnn_ln_gamma", "L0_gnn_ln_beta",
                                      "L1_gnn_forward_bias", "L1_gnn_backward_bias", "L1_gnn_self_bias")):
                v = a[name].rearrange("h c -> (h c)") if k < 2 else a[name]
                sp.dma_start(row[:, k, :], v.rearrange("(a n) -> a n", a=1)).then_inc(rows_in, 16)
            sp.dma_start(Wg[:, :, 0:D], a["L0_gnn_W"].rearrange("(c p) o -> p c o", p=P)).then_inc(w_in, 16)
            sp.dma_start(X[:, :, :], node_rows(a["x"])).then_inc(x_in, 16)
            sp.dma_start(Wl[:, :, :], a["L1_gnn_loop_weight"].rearrange("(c p) o -> p c o", p=P)).then_inc(w_in, 16)
            for d, names in enumerate((("dst", "src"), ("src", "dst"))):
                sp.wait_ge(made, d + 1)
                for buf, name in zip((own_i, oth_i, typ_i), (*names, "edge_type_16")):
                    sp.dma_start(buf[0:FULL, :], a[name][0:FULL * C0].rearrange("(p c) -> p c", c=C0)).then_inc(edges_in[d], 16)
                    sp.dma_start(buf[FULL:FULL + 1, 0:REST],
                                 a[name][FULL * C0:E].rearrange("(p c) -> p c", p=1)).then_inc(edges_in[d], 16)
                if d == 0:
                    sp.wait_ge(act_lin, 3 * NT)
                    sp.dma_start(node_rows(h_table), Hn[:, :, 0:HW]).then_inc(h_out, 16)
                    sp.wait_ge(tab_ready, 1)
                    sp.dma_start(node_rows(s_table), stab[:, :, :]).then_inc(s_out, 16)
            sp.wait_ge(sort_done, 2)
            for d, name in enumerate(("L1_gnn_Wf", "L1_gnn_Wb")):
                for c in range(2):
                    sp.dma_start(WV[:, d, :, c, :], a[name][:, c * P:(c + 1) * P, :].rearrange("r p o -> p r o")).then_inc(wr_in, 16)
            sp.wait_ge(tab_ready, 2)
            sp.dma_start(node_rows(x_table), X[:, :, :]).then_inc(x_out, 16)
            sp.wait_ge(out_ready, 1)
            sp.dma_start(node_rows(out), ACC[0][:, :, 0:D]).then_inc(out_done, 16)
            for f, dst in dbg.values():
                sp.dma_start(dst, f(loc)).then_inc(out_done, 16)
            sp.wait_ge(out_done, 16 + 16 * len(dbg))

        @block.gpsimd
        def _(pool):
            pool.iota(iota_i[:, :], [[1, T2]], base=0, channel_multiplier=0).then_inc(filled, 1)
            pool.iota(pidx_i[:, :], [[1, 1]], base=0, channel_multiplier=1).then_inc(filled, 1)
            pool.memset(identf[:, :], 0.0).then_inc(filled, 1)
            pool.memset(identb[:, :], 0.0).then_inc(filled, 1)
            pool.memset(trif[:, :], 1.0).then_inc(filled, 1)
            pool.memset(triif[:, :], 1.0).then_inc(filled, 1)
            pool.memset(sel[:, :, :], 0.0).then_inc(filled, 1)
            pool.memset(nbig[:, :, :], 0.0).then_inc(filled, 1)
            pool.wait_ge(filled, 8)
            for m in (identf, identb):
                pool.affine_select(out=m[:, :], in_=m[:, :], compare_op=ALU.not_equal, fill=1.0, base=0,
                                   pattern=[[-1, P]], channel_multiplier=1).then_inc(filled, 1)
            pool.affine_select(out=trif[:, :], in_=trif[:, :], compare_op=ALU.is_gt, fill=0.0, base=0,
                               pattern=[[1, P]], channel_multiplier=-1).then_inc(filled, 1)
            pool.affine_select(out=triif[:, :], in_=triif[:, :], compare_op=ALU.is_ge, fill=0.0, base=0,
                               pattern=[[1, P]], channel_multiplier=-1).then_inc(filled, 1)
            pool.affine_select(out=nbig[:, :, :], in_=nbig[:, :, :], compare_op=ALU.not_equal, fill=ABSENT, base=0,
                               pattern=[[0, G], [-1, P]], channel_multiplier=1).then_inc(filled, 1)
            for m in range(3):
                pool.affine_select(out=sel[:, :, :], in_=sel[:, :, :], compare_op=ALU.not_equal, fill=1.0, base=-H * m,
                                   pattern=[[-1, H], [0, P]], channel_multiplier=1).then_inc(filled, 1)
                pool.wait_ge(filled, 14 + m)

            gathered = 0
            for phase in range(4):
                if phase == 0:
                    pool.wait_ge(s_out, 16)
                elif phase == 1:
                    pool.wait_ge(h_out, 16)
                elif phase == 2:
                    pool.wait_ge(x_out, 16)
                slots = T1 if phase < 2 else T2
                first = PHASE_AT[phase]
                with pool.Fori(0, slots // 8) as i:
                    for u in range(8):
                        if u % G == 0:
                            pool.wait_ge(idx_ready, first // G + 2 * phase + 2 * i + u // G + 1)
                        pool.wait_ge(slot_free, first + 8 * i + u + 1)
                        pool.sem_inc(gate, 1)
                        if phase == 0:
                            dst, table = sring[:, u, :], s_table
                        elif phase == 1:
                            dst, table = ring[:, u, :], h_table
                        else:
                            dst, table = ring[:, u, 0:D], x_table
                        pool.indirect_dma_start(out=dst, out_offset=None, in_=table,
                                                in_offset=bass.IndirectOffsetOnAxis(ap=idxc[:, u:u + 1], axis=0)
                                                ).then_inc(gath[u], 16)

        @block.scalar
        def _(act):
            act.wait_ge(x_in, 16)
            with act.Fori(0, NT) as t:
                act.activation(xs[:, :], X[:, ds(t, 1), :].rearrange("p a f -> p (a f)"), ACT.Copy).then_inc(act_lin, 1)
                act.wait_ge(pe_lin, 2 * t + 1)
                act.activation(att[:, 0, 0:2 * NL], PS[:, 0, 0:2 * NL], ACT.Copy).then_inc(act_lin, 1)
                act.wait_ge(pe_lin, 2 * t + 2)
                act.sem_inc(gate, 1)
                act.activation(Hn[:, ds(t, 1), :].rearrange("p a f -> p (a f)"), PS[0:NL, 1, 0:XW], ACT.Copy).then_inc(act_lin, 1)

            def indices(phase, group, half):
                idx = idx1 if phase < 2 else idx2[phase - 2]
                act.activation(idxc[:, half * G:(half + 1) * G], idx[:, ds(group * G, G)], ACT.Copy).then_inc(idx_ready, 1)

            def gathers_done(phase, i, half):
                for u in range(half * G, (half + 1) * G):
                    act.wait_ge(gath[u], 16 * (PHASE_AT[phase] // 8 + i + 1))

            act.wait_ge(sort_done, 1)
            indices(0, 0, 0)
            indices(0, 1, 1)
            with act.Fori(0, T1 // 8) as i:
                for u in range(8):
                    act.wait_ge(turned, 8 * i + u + 1)
                    act.wait_ge(v_done, 8 * i + u + 1)
                    act.activation(asT[:, u % 2, :], PS[0:3 * H, 4 + u % 2, 0:P // 2].bitcast(bf16), ACT.Copy).then_inc(ast_ready, 1)
                    if u % G == G - 1:
                        gathers_done(0, i, u // G)
                        act.sem_inc(gate, 1)
                        indices(0, 2 * i + 2 + u // G, u // G)
            act.wait_ge(shift_ready, 1)
            act.activation(n1[:, :, :], n0[:, :, :], ACT.Exp).then_inc(self_exp, 1)
            act.wait_ge(idx_ready, T1 // G + 2)
            indices(1, 0, 0)
            indices(1, 1, 1)
            with act.Fori(0, T1 // 8) as i:
                for g in range(2):
                    act.wait_ge(oht_ps, 2 * i + g + 1)
                    act.wait_ge(adc_done, 8 * i + G * g + G)
                    act.activation(ohT[:, :, :], PS[0:NL, g, :].rearrange("p (u e) -> p u e", u=G), ACT.Copy).then_inc(oht_ready, 1)
                    act.wait_ge(z_ready, 2 * i + g + 1)
                    act.wait_ge(agg_done, 8 * i + G * g + G)
                    act.activation(scaled[:, :, D:HW], small[:, 0, :].rearrange("p (u h) -> p u h", u=G), ACT.Exp).then_inc(p_ready, 1)
                    gathers_done(1, i, g)
                    act.sem_inc(gate, 1)
                    indices(1, 2 * i + 2 + g, g)
            for k in range(2):
                act.wait_ge(ln_in, k + 1)
                act.activation(stat[:, :, 3], stat[:, :, 2], ACT.Sqrt).then_inc(ln_act, 1)
            for d in (0, 1):
                act.wait_ge(idx_ready, PHASE_AT[2 + d] // G + 2 * (2 + d))
                indices(2 + d, 0, 0)
                indices(2 + d, 1, 1)
                with act.Fori(0, T2 // 8) as i:
                    for g in range(2):
                        for b in range(2):
                            n = d * T2 + 8 * i + G * g + 2 * b
                            act.wait_ge(at_ps, n + 2)
                            act.wait_ge(y_done, n + 2)
                            act.activation(att[:, 2 * b:2 * b + 2, 0:2 * NL],
                                           PS[:, 2 * g + b, :].rearrange("p (u k) -> p u k", u=2)[:, :, 0:2 * NL],
                                           ACT.Copy).then_inc(at_ready, 2)
                        gathers_done(2 + d, i, g)
                        act.sem_inc(gate, 1)
                        indices(2 + d, 2 * i + 2 + g, g)
            with act.Fori(0, NT) as t:
                act.activation(xs[:, :], X[:, ds(t, 1), :].rearrange("p a f -> p (a f)"), ACT.Copy).then_inc(fin_act, 1)
                act.wait_ge(fin_ps, 2 * t + 1)
                act.activation(att[:, 0, 0:2 * NL], PS[:, 0, 0:2 * NL], ACT.Copy).then_inc(fin_act, 1)
                act.wait_ge(fin_ps, 2 * t + 2)
            act.wait_ge(ln_in, 3)
            act.activation(stat[:, :, 3], stat[:, :, 2], ACT.Sqrt).then_inc(ln_act, 1)

        @block.tensor
        def _(pe):
            def mm(*args, **kw):
                return pe.matmul(*args, **kw)

            pe.wait_ge(made, 1)
            pe.wait_ge(rows_in, 128)
            for k in range(4):
                for m in range(2):
                    last = mm(PS[:, 2 + k, m * D:(m + 1) * D], onesf[0:1, :], row[0:1, 2 * k + m, :], start=True, stop=True)
            last.then_inc(spread, 1)
            pe.wait_ge(wg_ready, 1)
            with pe.Fori(0, NT) as t:
                pe.wait_ge(act_lin, 3 * t + 1)
                for c in range(2):
                    last = pe.transpose(PS[:, 0, c * NL:(c + 1) * NL], xs[:, c * P:(c + 1) * P], identf[0:NL, 0:NL])
                last.then_inc(pe_lin, 1)
                pe.wait_ge(act_lin, 3 * t + 2)
                for c in range(2):
                    last = mm(PS[0:NL, 1, 0:XW], att[:, 0, c * NL:(c + 1) * NL], Wg[:, c, :], start=c == 0, stop=c == 1)
                last.then_inc(pe_lin, 1)
            pe.wait_ge(act_lin, 3 * NT)

            si, so = Steps(sort_in), Steps(sort_out)
            pi, po = Steps(perm_in), Steps(perm_out)

            def permute(cols, width):
                parts = width // T1 if width == T1 else 2
                w = width // parts
                pe.wait_ge(sort_in, si.step())
                for k in range(2):
                    for h in range(parts):
                        last = mm(PS[:, 4 + k * parts + h, 0:w], zero16[:, :], iota16[:, 0:w], start=True, stop=False)
                last.then_inc(perm_out, 4)
                po.base += 4
                with pe.Fori(0, cols // 4) as i:
                    for u in range(4):
                        pe.wait_ge(perm_in, pi.base + 4 * i + u + 1)
                        for k in range(2):
                            for h in range(parts):
                                last = mm(PS[:, 4 + k * parts + h, 0:w], lab[:, u, k, :], ohj[:, u, h * w:(h + 1) * w], start=False, stop=False)
                        last.then_inc(perm_out, 1)
                pi.base += cols
                for k in range(2):
                    for h in range(parts):
                        last = mm(PS[:, 4 + k * parts + h, 0:w], zero16[:, :], iota16[:, 0:w], start=False, stop=True)
                last.then_inc(perm_out, 1)

            for d in (0, 1):
                pe.wait_ge(sort_in, si.step())
                mm(PS[:, 2, 0:NT], onesf[:, :], rowtot, start=True, stop=True)
                mm(PS[:, 2, 32:32 + NT], trif[:, :], rowtot, start=True, stop=True)
                mm(PS[0:NT, 2, 64:65], rowtot, onesf[:, 0:1], start=True, stop=True).then_inc(sort_out, 1)
                pe.wait_ge(sort_in, si.step())
                mm(PS[0:NT, 2, 65:66], triif[0:NT, 0:NT], c1[0:NT, :], start=True, stop=True).then_inc(sort_out, 1)
                pe.wait_ge(sort_in, si.step())
                mm(PS[:, 3, 0:T1], ones16[0:NT, :], cmp16[0:NT, 0:T1], start=True, stop=True).then_inc(sort_out, 1)
                permute(C0, T1)
                pe.wait_ge(sort_in, si.step())
                with pe.Fori(0, R) as t:
                    for k in range(4):
                        last = mm(PS[0:T1 // 4, 2, ds(t + 16 * k, 1)], masks[:, ds(t, 1), k * (T1 // 4):(k + 1) * (T1 // 4)].rearrange("p a j -> p (a j)"),
                                  ones16[:, 0:1], start=True, stop=True)
                last = mm(PS[0:1, 2, 64:65], ones16[:, 0:1], ones16[:, 0:1], start=True, stop=True)
                last.then_inc(sort_out, 1)
                pe.wait_ge(sort_in, si.step())
                for k in range(4):
                    last = mm(PS[0:NT, 2, 128:128 + R], dT[0:T1 // 4, k * NT:(k + 1) * NT], cntj[0:T1 // 4, k * R:(k + 1) * R], start=k == 0, stop=k == 3)
                last.then_inc(sort_out, 1)
                pe.wait_ge(sort_in, si.step())
                mm(PS[0:NT, 2, 160:160 + R], trif[0:NT, 0:NT], cnt[0:NT, :], start=True, stop=True)
                mm(PS[0:NT, 2, 176:177], trif[0:NT, 0:NT], end2[0:NT, R - 1:R], start=True, stop=True).then_inc(sort_out, 1)
                for t in range(R):
                    pe.wait_ge(sort_in, si.step())
                    for h in range(2):
                        last = mm(PS[:, h, 0:T2 // 2], ones16[0:NT, :], cmp16[0:NT, h * (T2 // 2):(h + 1) * (T2 // 2)], start=t == 0, stop=t == R - 1)
                        if t == R - 1:
                            last = mm(PS[:, 4 + h, 0:T2 // 2], ones16[0:NT, :], cmp16[0:NT, h * (T2 // 2):(h + 1) * (T2 // 2)], start=True, stop=True)
                    last.then_inc(sort_out, 1)
                a0 = si.base
                with pe.Fori(0, R) as t:
                    pe.wait_ge(sort_in, a0 + t + 1)
                    mm(PS[:, 2, 0:T1], tri16[:, :], masks[:, ds(t, 1), :].rearrange("p a j -> p (a j)"), start=True, stop=False)
                    mm(PS[:, 2, 0:T1], shiftb[0:NT, :], dmap[0:NT, :], start=False, stop=True)
                    mm(PS[:, 3, 0:T1], ones16[:, :], masks[:, ds(t, 1), :].rearrange("p a j -> p (a j)"), start=True, stop=True).then_inc(sort_out, 1)
                si.base += R
                permute(T1, T2)

            pe.wait_ge(sort_done, 2)
            pe.sem_inc(v_done, 2)

            def turn(i, u):
                pe.wait_ge(gath[u], 16 * (i + 1))
                pe.wait_ge(ast_ready, 8 * i + u + 1 - 2 if isinstance(i, int) and 8 * i + u >= 2 else 8 * i + u - 1) if not (isinstance(i, int) and 8 * i + u < 2) else None
                pe.transpose(PS[0:3 * H, 4 + u % 2, 0:P // 2].bitcast(bf16), sring[:, u, :], identb[:, :]).then_inc(turned, 1)
                pe.wait_ge(turned, 8 * i + u + 1)
                pe.sem_inc(slot_free, 1)

            def values(i, u):
                pe.wait_ge(noh_ready, 8 * i + u + 1)
                pe.wait_ge(ast_ready, 8 * i + u + 1)
                pe.wait_ge(max_taken, 8 * i + u + 1)
                for b in range(2):
                    mm(PS[0:NL, (u % 2) * 2 + b, :], noh[:, u % 4, :], nbig[:, :, :].rearrange("p a b -> p (a b)"), start=True, stop=False)
                for h in range(H):
                    last = mm(PS[0:NL, (u % 2) * 2 + h // 4, (h % 4) * P:(h % 4 + 1) * P], sel[:, h, 0:NL], asT[:, u % 2, :],
                              start=False, stop=h % 4 == 3)
                last.then_inc(v_done, 1)

            turn(0, 0)
            for u in range(8):
                if u < 7:
                    turn(0, u + 1)
                else:
                    turn(1, 0)
                values(0, u)
            with pe.Fori(1, T1 // 8 - 1) as i:
                for u in range(8):
                    if u < 7:
                        turn(i, u + 1)
                    else:
                        turn(i + 1, 0)
                    values(i, u)
            for u in range(8):
                if u < 7:
                    turn(T1 // 8 - 1, u + 1)
                values(T1 // 8 - 1, u)

            pe.wait_ge(shift_ready, 1)
            pe.sem_inc(adc_done, G)
            pe.sem_inc(agg_done, G)
            with pe.Fori(0, T1 // 8) as i:
                for g in range(2):
                    tiles = []
                    for u in range(G):
                        n = 8 * i + G * g + u
                        pe.wait_ge(oh_ready, n + 1)
                        last = pe.transpose(PS[0:NL, g, u * P:(u + 1) * P], oh[:, G * g + u, :], identf[:, :])
                    last.then_inc(oht_ps, 1)
                    pe.wait_ge(oht_ready, 2 * i + g + 1)
                    for u in range(G):
                        n = 8 * i + G * g + u
                        t = pe.value_load(tile1[0:1, ds(n, 1)], min_val=0, max_val=NT - 1)
                        mm(PS[:, 2, u * 2 * H:(u + 1) * 2 * H], ohT[:, u, :], ADC[:, ds(t, 1), :].rearrange("p a k -> p (a k)"), start=True, stop=True).then_inc(adc_done, 1)
                    for u in range(G):
                        n = 8 * i + G * g + u
                        pe.wait_ge(hp_ready, n + 1)
                        pe.wait_ge(acc_taken, n + 1)
                        mm(PS[0:NL, 3 + u, 0:HW], oh[:, G * g + u, :], scaled[:, u, :], start=True, stop=True).then_inc(agg_done, 1)

            pe.wait_ge(wr_in, 64)
            pe.sem_inc(y_done, G)
            for d in (0, 1):
                with pe.Fori(0, T2 // 8) as i:
                    for g in range(2):
                        for u in range(G):
                            n = d * T2 + 8 * i + G * g + u
                            b = g * 2 + u // 2
                            pe.wait_ge(gath[G * g + u], 16 * (PHASE_AT[2 + d] // 8 + i + 1))
                            pe.wait_ge(moh_ready, n + 1)
                            for c in range(2):
                                last = mm(PS[:, b, (u % 2) * 256 + c * NL:(u % 2) * 256 + (c + 1) * NL],
                                          ring[:, G * g + u, c * P:(c + 1) * P], oh[:, G * g + u, :], start=True, stop=True)
                            last.then_inc(at_ps, 1)
                        for u in range(G):
                            n = d * T2 + 8 * i + G * g + u
                            r = pe.value_load(rel2[d][0:1, ds(8 * i + G * g + u, 1)], min_val=0, max_val=R - 1)
                            pe.wait_ge(at_ready, n + 1)
                            pe.wait_ge(y_taken, n + 1)
                            for c in range(2):
                                mm(PS[0:NL, 4 + u, 0:D], att[:, u, c * NL:(c + 1) * NL], WV[:, d, ds(r, 1), c, :].rearrange("p a o -> p (a o)"), start=c == 0, stop=c == 1)
                            mm(PS[0:NL, 4 + u, D:D + 1], oh[:, G * g + u, :], onesf[:, 0:1], start=True, stop=True).then_inc(y_done, 1)
                            pe.wait_ge(y_done, G + n + 1)
                            pe.sem_inc(slot_free, 1)
            with pe.Fori(0, NT) as t:
                pe.wait_ge(fin_act, 2 * t + 1)
                for c in range(2):
                    last = pe.transpose(PS[:, 0, c * NL:(c + 1) * NL], xs[:, c * P:(c + 1) * P], identf[0:NL, 0:NL])
                last.then_inc(fin_ps, 1)
                pe.wait_ge(fin_act, 2 * t + 2)
                pe.wait_ge(fin_taken, t + 1)
                for c in range(2):
                    last = mm(PS[0:NL, 1, 0:D], att[:, 0, c * NL:(c + 1) * NL], Wl[:, c, :], start=c == 0, stop=c == 1)
                last.then_inc(fin_ps, 1)

        @block.vector
        def _(dve):
            S = Steps(vs)

            def v(ins):
                ins.then_inc(vs, 1)
                dve.wait_ge(vs, S.step())

            def ts(out, in_, s1, op0, s2=None, op1=ALU.bypass, **kw):
                return dve.tensor_scalar(out, in_, s1, s2, op0, op1, **kw)

            def stt(out, in0, s, in1, op0, op1):
                return dve.scalar_tensor_tensor(out=out, in0=in0, scalar=s, in1=in1, op0=op0, op1=op1)

            cp, tt = dve.tensor_copy, dve.tensor_tensor

            v(dve.memset(ones16[:, :], 1.0))
            v(dve.memset(onesf[:, :], 1.0))
            v(dve.memset(onesw[:, :], 1.0))
            v(dve.memset(zero16[:, :], 0.0))
            for idx, w in ((idx1, T1), (idx2[0], T2), (idx2[1], T2)):
                v(dve.memset(idx[:, w:w + 2 * G], 0))
            v(dve.memset(own_i, 4000))
            v(dve.memset(oth_i, 0))
            v(dve.memset(typ_i, 0))
            dve.wait_ge(filled, 16)
            v(cp(iota16[:, :], iota_i[:, :]))
            v(cp(iotaf[:, :], iota_i[:, 0:P]))
            v(cp(pidx[:, :], pidx_i[:, :]))
            v(cp(tri16[:, :], trif[:, :]))
            dve.sem_inc(made, 1)
            prod = scaled[:, 0:2, 0:D]
            dve.wait_ge(spread, 1)
            v(cp(bc[:, :, :], PS[:, 2:6, :].rearrange("p b (k f) -> p (b k) f", k=2)))
            dve.wait_ge(w_in, 32)
            for k in range(2):
                v(tt(prod, Wg[:, :, 0:D],
                     bc[:, k:k + 1, :].broadcast_to([P, 2, D]), ALU.mult))
                v(dve.reduce_sum(Wg[:, :, D + k * H:D + (k + 1) * H],
                                 prod.rearrange("p c (h f) -> p c h f", h=H), AX.X))
            dve.sem_inc(wg_ready, 1)

            so = Steps(sort_out)
            perm = [0, 0]

            def ask():
                dve.sem_inc(sort_in, 1)
                dve.wait_ge(sort_out, so.step())

            def split(width, p):
                v(cp(t0[:, 0:width].bitcast(i32), p))
                v(ts(t1[:, 0:width].bitcast(i32), t0[:, 0:width].bitcast(i32), 7, ALU.logical_shift_right))
                v(ts(t2[:, 0:width].bitcast(i32), t0[:, 0:width].bitcast(i32), P - 1, ALU.bitwise_and))
                v(cp(jf[:, 0:width], t1[:, 0:width].bitcast(i32)))
                v(cp(sf[:, 0:width], t2[:, 0:width].bitcast(i32)))

            def permute(cols, width, va, vb):
                dve.sem_inc(sort_in, 1)
                with dve.Fori(0, cols // 4) as i:
                    for u in range(4):
                        c = i * 4 + u
                        dve.wait_ge(perm_out, perm[1] + 4 * i + u + 1)
                        ts(ohj[:, u, 0:width], iota16[:, 0:width], jf[:, ds(c, 1)], ALU.is_equal)
                        ts(lab[:, u, 0, :], iota16[:, 0:P], sf[:, ds(c, 1)], ALU.is_equal, va[:, ds(c, 1)], ALU.mult)
                        ts(lab[:, u, 1, :], iota16[:, 0:P], sf[:, ds(c, 1)], ALU.is_equal, vb[:, ds(c, 1)], ALU.mult).then_inc(perm_in, 1)
                perm[1] += 4 + cols + 1
                dve.wait_ge(perm_out, perm[1])

            def slots_of(dst, src):
                v(cp(dst.bitcast(i32), src))
                v(ts(dst.bitcast(i32), dst.bitcast(i32), P - 1, ALU.add))
                v(ts(dst.bitcast(i32), dst.bitcast(i32), 7, ALU.logical_shift_right))

            for d in (0, 1):
                E0 = slice(0, C0)
                dve.wait_ge(edges_in[d], 96)
                v(cp(hi[:, E0], own_i))
                v(cp(Av[:, E0], oth_i))
                v(cp(Bv[:, E0], typ_i))
                v(ts(t0[:, E0], hi[:, E0], 1.0 / NL, ALU.mult, 0.5 / NL - 0.5, ALU.add))
                v(cp(jf[:, E0].bitcast(i32), t0[:, E0]))
                v(cp(t0[:, E0], jf[:, E0].bitcast(i32)))
                v(stt(t1[:, E0], t0[:, E0], -float(NL), hi[:, E0], ALU.mult, ALU.add))
                v(ts(t2[:, E0], t1[:, E0], float(NL), ALU.is_ge))
                v(ts(pos[:, E0], t1[:, E0], 0.0, ALU.is_lt))
                v(tt(t2[:, E0], t2[:, E0], pos[:, E0], ALU.subtract))
                v(tt(hi[:, E0], t0[:, E0], t2[:, E0], ALU.add))
                v(stt(lo[:, E0], t2[:, E0], -float(NL), t1[:, E0], ALU.mult, ALU.add))
                v(ts(lo[:, E0], lo[:, E0], 1.0, ALU.add, 16.0, ALU.mult))
                v(tt(Bv[:, E0], Bv[:, E0], lo[:, E0], ALU.add))
                v(ts(Av[:, E0], Av[:, E0], -float(OFF), ALU.add))
                if d == 0:
                    dve.wait_ge(edges_in[0], 96)
                with dve.Fori(0, NT) as b:
                    S.loop(b, 1)
                    v(ts(t0[:, E0], hi[:, E0], iotaf[:, ds(b, 1)], ALU.is_equal, None, ALU.add, accum_out=rowtot[:, ds(b, 1)]))
                S.end(NT)
                ask()
                slots_of(r1, PS[:, 2, 0:NT])
                v(cp(offs, r1.bitcast(i32)))
                v(ts(r1, offs, 1.0, ALU.mult))
                v(dve.tensor_tensor_scan(r0, onesf[:, 0:NT], r1, 0.0, ALU.mult, ALU.add))
                v(tt(offs, r0, r1, ALU.subtract))
                v(stt(offs, offs, float(P), PS[:, 2, 32:32 + NT], ALU.mult, ALU.add))
                v(ts(offs, offs, -1.0, ALU.add))
                slots_of(c0[0:NT, :], PS[0:NT, 2, 64:65])
                v(cp(c1[0:NT, :], c0[0:NT, :].bitcast(i32)))
                ask()
                v(cp(c2[0:NT, :], PS[0:NT, 2, 65:66]))
                v(ts(cmp16[0:NT, 0:T1], iota16[0:NT, 0:T1], c2[0:NT, :], ALU.is_ge))
                ask()
                v(ts(q0[:, 0:T1], PS[:, 3, 0:T1], float(NT - 1), ALU.min))
                if d == 0:
                    v(cp(tile1[:, :], q0[:, 0:T1]))
                v(ts(dmap[0:NT, :], q0[0:NT, 0:T1], pidx[0:NT, :], ALU.is_equal))
                v(ts(pos[:, E0], hi[:, E0], float(NT), ALU.is_ge, FAR, ALU.mult))
                with dve.Fori(0, NT) as b:
                    S.loop(b, 4)
                    v(ts(t0[:, E0], hi[:, E0], iotaf[:, ds(b, 1)], ALU.is_equal))
                    v(dve.tensor_tensor_scan(t1[:, E0], onesw[:, E0], t0[:, E0], offs[:, ds(b, 1)], ALU.mult, ALU.add))
                    v(tt(t1[:, E0], t1[:, E0], t0[:, E0], ALU.mult))
                    v(tt(pos[:, E0], pos[:, E0], t1[:, E0], ALU.add))
                S.end(NT)
                split(C0, pos[:, E0])
                permute(C0, T1, Av, Bv)
                v(cp(A1, PS[:, 4, 0:T1]))
                v(cp(B1, PS[:, 5, 0:T1]))
                v(cp(t0.bitcast(i32), B1))
                v(ts(t1.bitcast(i32), t0.bitcast(i32), 4, ALU.logical_shift_right))
                v(ts(t2.bitcast(i32), t0.bitcast(i32), R - 1, ALU.bitwise_and))
                v(cp(lo, t1.bitcast(i32)))
                v(cp(typ1, t2.bitcast(i32)))
                if d == 0:
                    v(ts(idx1[:, 0:T1], A1, float(OFF), ALU.add))
                    v(cp(lo1[:, :], lo))
                v(ts(t0, lo, 0.0, ALU.is_equal, 99.0, ALU.mult))
                v(tt(typ1, typ1, t0, ALU.add))
                with dve.Fori(0, R) as t:
                    S.loop(t, 1)
                    v(ts(masks[:, ds(t, 1), :].rearrange("p a j -> p (a j)"), typ1, iotaf[:, ds(t, 1)], ALU.is_equal))
                S.end(R)
                ask()
                q4 = T1 // 4
                v(cp(cntj[0:q4, :], PS[0:q4, 2, 0:4 * R]))
                for k in range(4):
                    v(ts(c3[0:q4, :], pidx[0:q4, :], float(q4 * k), ALU.add))
                    v(ts(q1[0:q4, 0:NT], r0[0:q4, :], c3[0:q4, :], ALU.is_le, None, ALU.add, accum_out=c0[0:q4, :]))
                    v(ts(c0[0:q4, :], c0[0:q4, :], float(NT - 1), ALU.min))
                    v(ts(dT[0:q4, k * NT:(k + 1) * NT], iotaf[0:q4, 0:NT], c0[0:q4, :], ALU.is_equal))
                ask()
                v(cp(cnt[0:NT, :], PS[0:NT, 2, 128:128 + R]))
                slots_of(s0[0:NT, :], cnt[0:NT, :])
                v(cp(s1[0:NT, :], s0[0:NT, :].bitcast(i32)))
                v(dve.tensor_tensor_scan(end2[0:NT, :], onesf[0:NT, 0:R], s1[0:NT, :], 0.0, ALU.mult, ALU.add))
                ask()
                v(cp(c2[0:NT, :], PS[0:NT, 2, 176:177]))
                v(ts(end2[0:NT, :], end2[0:NT, :], c2[0:NT, :], ALU.add))
                v(tt(shift[0:NT, :], end2[0:NT, :], s1[0:NT, :], ALU.subtract))
                v(stt(shift[0:NT, :], shift[0:NT, :], float(P), PS[0:NT, 2, 160:160 + R], ALU.mult, ALU.subtract))
                for t in range(R):
                    v(ts(cmp16[0:NT, :], iota16[0:NT, :], end2[0:NT, t:t + 1], ALU.is_ge))
                    ask()
                halves = lambda x: x.rearrange("p (h j) -> p h j", h=2)
                v(ts(halves(q0), PS[:, 4:6, 0:T2 // 2], float(NT - 1), ALU.min))
                v(ts(halves(q1), PS[:, 0:2, 0:T2 // 2], float(NT * R - 1), ALU.min))
                v(stt(q1, q0, -float(R), q1, ALU.mult, ALU.add))
                v(cp(tile2[d], q0[64 * d:64 * d + 1, :]))
                v(cp(rel2[d], q1[64 * d + 32:64 * d + 33, :]))
                v(ts(pos, typ1, float(R), ALU.is_ge, FAR, ALU.mult))
                v(dve.memset(t2[:, 0:1], 0.0))
                s_in = so.base
                with dve.Fori(0, R) as t:
                    S.loop(t, 5)
                    v(ts(shiftb[0:NT, :], onesf[0:NT, :], shift[0:NT, ds(t, 1)], ALU.mult))
                    dve.sem_inc(sort_in, 1)
                    dve.wait_ge(sort_out, s_in + t + 1)
                    v(dve.tensor_tensor_scan(t2[:, 1:T1], onesw[:, 0:T1 - 1], PS[:, 3, 0:T1 - 1], 0.0, ALU.mult, ALU.add))
                    v(tt(t0, t2, PS[:, 2, 0:T1], ALU.add))
                    v(tt(t0, t0, masks[:, ds(t, 1), :].rearrange("p a j -> p (a j)"), ALU.mult))
                    v(tt(pos, pos, t0, ALU.add))
                S.end(R)
                so.base += R
                split(T1, pos)
                permute(T1, T2, A1, B1)
                v(ts(halves(idx2[d][:, 0:T2]), PS[:, 4:6, 0:T2 // 2], float(OFF), ALU.add))
                v(cp(halves(q0).bitcast(i32), PS[:, 6:8, 0:T2 // 2]))
                v(ts(q1.bitcast(i32), q0.bitcast(i32), 4, ALU.logical_shift_right))
                v(cp(lo2[d][:, :], q1.bitcast(i32)))
                if d == 0:
                    v(dve.memset(own_i, 4000))
                    v(dve.memset(oth_i, 0))
                    v(dve.memset(typ_i, 0))
                    dve.sem_inc(made, 1)
                    dve.wait_ge(act_lin, 3 * NT)
                    src_ = Hn[:, :, D:HW]
                    v(cp(stab[:, :, 0:H], src_))
                    v(tt(n0[:, :, :], src_, stab[:, :, 0:H], ALU.subtract))
                    v(cp(stab[:, :, H:2 * H], n0[:, :, :]))
                    v(tt(n0[:, :, :], n0[:, :, :], stab[:, :, H:2 * H], ALU.subtract))
                    v(cp(stab[:, :, 2 * H:3 * H], n0[:, :, :]))
                    dve.sem_inc(tab_ready, 1)
                    v(cp(M[:, :, :], src_))
                dve.sem_inc(sort_done, 1)

            dve.sem_inc(slot_free, 8)
            dve.sem_inc(max_taken, 2)

            def absent(j, u, n):
                if not isinstance(n, int) or n >= 4:
                    dve.wait_ge(v_done, n - 1)
                ts(noh[:, u % 4, :], iota16[:, 1:NL + 1], lo1[:, ds(j, 1)], ALU.not_equal).then_inc(noh_ready, 1)

            def taken(n, u):
                dve.wait_ge(v_done, n + 3)
                v(dve.reduce_max(mx[:, :], PS[0:NL, (u % 2) * 2:(u % 2) * 2 + 2, :].rearrange("p b (h e) -> p (b h) e", h=4), AX.X))
                dve.sem_inc(max_taken, 1)
                t = dve.value_load(tile1[0:1, ds(n, 1)], min_val=0, max_val=NT - 1)
                m = M[:, ds(t, 1), :].rearrange("p a h -> p (a h)")
                v(tt(m, m, mx[:, :], ALU.max))

            for u in range(2):
                absent(u, u, u)
            for u in range(6):
                absent(u + 2, u + 2, u + 2)
                taken(u, u)
            with dve.Fori(0, T1 // 8 - 1) as i:
                S.loop(i, 16)
                for u in range(8):
                    absent(8 * i + 8 + u, u, 8 * i + 8 + u)
                    taken(8 * i + 6 + u, (6 + u) % 8)
            S.end(T1 // 8 - 1)
            for u in range(2):
                taken(T1 - 2 + u, u)

            a_src, a_dst = Hn[:, :, D:HW], Hn[:, :, HW:XW]
            v(tt(n0[:, :, :], M[:, :, :], a_dst, ALU.add))
            v(stt(ADC[:, :, H:2 * H], n0[:, :, :], 0.2, n0[:, :, :], ALU.mult, ALU.max))
            v(cp(ADC[:, :, 0:H], a_dst))
            v(tt(n0[:, :, :], a_src, a_dst, ALU.add))
            v(stt(n0[:, :, :], n0[:, :, :], 0.2, n0[:, :, :], ALU.mult, ALU.max))
            v(tt(n0[:, :, :], n0[:, :, :], ADC[:, :, H:2 * H], ALU.subtract))
            dve.sem_inc(shift_ready, 1)
            dve.wait_ge(self_exp, 1)
            with dve.Fori(0, NT) as t:
                S.loop(t, 1)
                v(tt(ACC[0][:, ds(t, 1), 0:D].rearrange("p a (h c) -> p (a h) c", h=H), Hn[:, ds(t, 1), 0:D].rearrange("p a (h c) -> p (a h) c", h=H),
                     n1[:, ds(t, 1), :].rearrange("p a (h o) -> p (a h) o", o=1).broadcast_to([NL, H, HC]), ALU.mult))
            S.end(NT)
            v(cp(ACC[0][:, :, D:HW], n1[:, :, :]))

            dve.sem_inc(acc_taken, G)

            def onehots(i, g, lo_, k0, ready):
                for u in range(G):
                    n = 8 * i + G * g + u
                    ts(oh[:, G * g + u, :], iota16[:, 1:NL + 1], lo_[:, ds(n, 1)], ALU.is_equal).then_inc(ready, 1)

            def add_up(n, u, tiles, done, credit, width, acc, taken_, at0):
                dve.wait_ge(done, at0 + n + credit + 1)
                t = dve.value_load(tiles[0:1, ds(n, 1)], min_val=0, max_val=NT - 1)
                m = acc[:, ds(t, 1), 0:width].rearrange("p a f -> p (a f)")
                dve.tensor_tensor(m, m, PS[0:NL, u, 0:width], ALU.add).then_inc(taken_, 1)

            def attend(i, g, first):
                n0_ = 8 * i + G * g
                onehots(i, g, lo1, 0, oh_ready)
                if not first:
                    for u in range(G):
                        if not (isinstance(n0_, int) and n0_ == 0):
                            dve.wait_ge(acc_taken, n0_ - G + u + G)
                        add_up(n0_ - G + u, 3 + u, tile1, agg_done, G, HW, ACC[0], acc_taken, 0)
                dve.wait_ge(adc_done, n0_ + 2 * G)
                for u in range(G):
                    dve.wait_ge(gath[G * g + u], 16 * (PHASE_AT[1] // 8 + i + 1))
                adc = PS[:, 2, 0:2 * H * G].rearrange("p (u k) -> p u k", u=G)
                z = [small[:, k, :].rearrange("p (u h) -> p u h", u=G) for k in range(4)]
                v(tt(z[1], ring[:, G * g:G * g + G, D:HW], adc[:, :, 0:H], ALU.add))
                v(stt(z[2], z[1], 0.2, z[1], ALU.mult, ALU.max))
                v(tt(z[3], z[2], adc[:, :, H:2 * H], ALU.subtract))
                v(ts(z[0], z[3], 0.0, ALU.min))
                dve.sem_inc(z_ready, 1)
                dve.wait_ge(p_ready, 2 * i + g + 1)
                for u in range(G):
                    tt(scaled[:, u, 0:D].rearrange("p (h c) -> p h c", h=H), ring[:, G * g + u, 0:D].rearrange("p (h c) -> p h c", h=H),
                       scaled[:, u, D:HW].rearrange("p (h o) -> p h o", o=1).broadcast_to([P, H, HC]), ALU.mult).then_inc(hp_ready, 1)
                dve.wait_ge(hp_ready, n0_ + G)
                dve.sem_inc(slot_free, G)

            attend(0, 0, True)
            attend(0, 1, False)
            with dve.Fori(1, T1 // 8) as i:
                S.loop(i - 1, 8)
                attend(i, 0, False)
                attend(i, 1, False)
            S.end(T1 // 8 - 1)
            for u in range(G):
                dve.wait_ge(acc_taken, T1 - G + u + G)
                add_up(T1 - G + u, 3 + u, tile1, agg_done, G, HW, ACC[0], acc_taken, 0)
            dve.wait_ge(acc_taken, T1 + G)

            def layer_norm(src_, junk, to, gamma, k):
                mean, var = stat[:, :, 0:1], stat[:, :, 2:3]
                v(dve.reduce_sum(stat[:, :, 0], src_, AX.X))
                v(ts(stat[:, :, 0], stat[:, :, 0], 1.0 / D, ALU.mult))
                v(tt(src_, src_, mean.broadcast_to([NL, NT, D]), ALU.subtract))
                v(tt(junk, src_, src_, ALU.mult))
                v(dve.reduce_sum(stat[:, :, 1], junk, AX.X))
                v(ts(stat[:, :, 2], stat[:, :, 1], 1.0 / D, ALU.mult, LN_EPS, ALU.add))
                dve.sem_inc(ln_in, 1)
                dve.wait_ge(ln_act, k)
                v(dve.reciprocal(stat[:, :, 1], stat[:, :, 3]))
                v(tt(to, src_, stat[:, :, 1:2].broadcast_to([NL, NT, D]), ALU.mult))

            def vec(k):
                return bc[0:NL, k:k + 1, :].broadcast_to([NL, NT, D])

            o, j = ACC[0][:, :, 0:D], ACC[1][:, :, 0:D]
            v(ts(n0[:, :, :], ACC[0][:, :, D:HW], 1e-16, ALU.add))
            v(dve.reciprocal(n1[:, :, :], n0[:, :, :]))
            with dve.Fori(0, NT) as t:
                S.loop(t, 1)
                oo = ACC[0][:, ds(t, 1), 0:D].rearrange("p a (h c) -> p (a h) c", h=H)
                v(tt(oo, oo, n1[:, ds(t, 1), :].rearrange("p a (h o) -> p (a h) o", o=1).broadcast_to([NL, H, HC]), ALU.mult))
            S.end(NT)
            v(tt(o, o, vec(2), ALU.add))
            layer_norm(o, j, o, None, 1)
            v(tt(o, o, vec(3), ALU.mult))
            v(tt(o, o, vec(4), ALU.add))
            v(tt(o, o, X[:, :, :], ALU.add))
            layer_norm(o, j, X[:, :, :], None, 2)
            dve.sem_inc(tab_ready, 1)

            for d in (0, 1):
                v(dve.memset(ACC[d][:, :, 0:D + 1], 0.0))
            dve.sem_inc(y_taken, G)
            for d in (0, 1):
                def relate(i, g, first):
                    n0_ = 8 * i + G * g
                    onehots(i, g, lo2[d], d, moh_ready)
                    if not first:
                        for u in range(G):
                            dve.wait_ge(y_taken, d * T2 + n0_ + u)
                            add_up(n0_ - G + u, 4 + u, tile2[d], y_done, G, D + 1, ACC[d], y_taken, d * T2)

                relate(0, 0, True)
                relate(0, 1, False)
                with dve.Fori(1, T2 // 8) as i:
                    relate(i, 0, False)
                    relate(i, 1, False)
                for u in range(G):
                    dve.wait_ge(y_taken, d * T2 + T2 + u)
                    add_up(T2 - G + u, 4 + u, tile2[d], y_done, G, D + 1, ACC[d], y_taken, d * T2)
                dve.wait_ge(y_taken, (d + 1) * T2 + G)

            for d in (0, 1):
                deg = ACC[d][:, :, D:D + 1]
                v(ts(stat[:, :, 0:1], deg, 1.0, ALU.max))
                v(dve.reciprocal(stat[:, :, 1:2], stat[:, :, 0:1]))
                v(ts(stat[:, :, 2:3], deg, 1.0, ALU.min))
                v(tt(ACC[d][:, :, 0:D], ACC[d][:, :, 0:D], stat[:, :, 1:2].broadcast_to([NL, NT, D]), ALU.mult))
                with dve.Fori(0, NT) as t:
                    S.loop(t, 1)
                    m = ACC[d][:, ds(t, 1), 0:D].rearrange("p a f -> p (a f)")
                    v(stt(m, bc[0:NL, 5 + d, :], stat[:, ds(t, 1), 2:3].rearrange("p a o -> p (a o)"), m, ALU.mult, ALU.add))
                S.end(NT)
            v(tt(o, o, j, ALU.add))
            v(tt(o, o, vec(7), ALU.add))
            v(tt(o, o, X[:, :, :], ALU.add))
            dve.sem_inc(fin_taken, 1)
            with dve.Fori(0, NT) as t:
                S.loop(t, 1)
                dve.wait_ge(fin_ps, 2 * t + 2)
                m = ACC[0][:, ds(t, 1), 0:D].rearrange("p a f -> p (a f)")
                v(stt(m, PS[0:NL, 1, 0:D], 2.0, m, ALU.mult, ALU.add))
                dve.sem_inc(fin_taken, 1)
            S.end(NT)
            layer_norm(o, j, o, None, 3)
            dve.sem_inc(out_ready, 1)


PHASE_AT = [0, T1, 2 * T1, 2 * T1 + T2]

NAMES = ("x", "src", "dst", "edge_type_16", "L0_gnn_W", "L0_gnn_att_src", "L0_gnn_att_dst", "L0_gnn_bias", "L0_gnn_ln_gamma",
         "L0_gnn_ln_beta", "L1_gnn_Wf", "L1_gnn_Wb", "L1_gnn_loop_weight", "L1_gnn_forward_bias", "L1_gnn_backward_bias",
         "L1_gnn_self_bias")


def kernel(**inputs):
    import concourse.bacc as bacc
    from concourse.bass_utils import run_bass_kernel_spmd

    nc = bacc.Bacc("TRN2", target_bir_lowering=False, num_devices=1)
    arrays, aps = {}, {}
    for name in NAMES:
        arrays[name] = np.ascontiguousarray(inputs[name])
        aps[name] = nc.dram_tensor(name, arrays[name].shape, mybir.dt.from_np(arrays[name].dtype), kind="ExternalInput").ap()
    out = nc.dram_tensor("result", (N, D), f32, kind="ExternalOutput").ap()
    build_program(nc, aps, out)
    ran = run_bass_kernel_spmd(nc, [arrays], core_ids=[0])
    return ran.results[0]["result"]
```

```python
import numpy as np
import concourse.bass as bass
from concourse import mybir
from contextlib import ExitStack

ARENA = 6400
P = 128
N, D, H, R = 3125, 256, 8, 16
HC = D // H
E = 50000
NL = 125
NT = N // NL
C0 = 392
FULL = E // C0
REST = E - FULL * C0
T1 = 416
T2 = 792
assert T1 * P >= E + (P - 1) * NT and T2 * P >= E + (P - 1) * NT * R
HW = D + H
XW = D + 2 * H
G = 4
OFF = 1600
NONE = N
FAR = 128.0 * 1024
ABSENT = -(2.0 ** 100)
LN_EPS = 1e-5

f32, f16, bf16 = mybir.dt.float32, mybir.dt.float16, mybir.dt.bfloat16
i16, i32 = mybir.dt.int16, mybir.dt.int32
ALU = mybir.AluOpType
ACT = mybir.ActivationFunctionType
AX = mybir.AxisListType
ds = bass.ds


class Steps:

    def __init__(self, sem):
        self.sem, self.base, self.k, self.i, self.per = sem, 0, 0, None, 0

    def loop(self, i, per):
        self.i, self.per, self.k = i, per, 0

    def end(self, times):
        assert self.k == self.per, (self.k, self.per)
        self.base += self.per * times
        self.i, self.k = None, 0

    @property
    def now(self):
        if self.i is None:
            return self.base
        return self.base + self.i * self.per + self.k

    def step(self):
        if self.i is None:
            self.base += 1
        else:
            self.k += 1
        return self.now


def build_program(nc, a, out):
    ctx = ExitStack()
    with ctx:
        def sb(name, shape, dt=f32):
            return ctx.enter_context(nc.sbuf_tensor(name, shape, dt))

        def sem(name):
            return ctx.enter_context(nc.semaphore(name))

        h_table = nc.dram_tensor("h_table", (N + 1, HW), f32).ap()
        s_table = nc.dram_tensor("s_table", (N + 1, 3 * H), bf16).ap()
        x_table = nc.dram_tensor("x_table", (N, 3 * D), bf16).ap()

        X = sb("X", [NL, NT, D])
        ACC = [sb("ACC0", [NL, NT, HW]), sb("ACC1", [NL, NT, XW])]
        Hn = ACC[1]
        WR = sb("WR", [P, 2 * R * 2 * D])
        bc = sb("bc", [P, 8, D])
        Wg = sb("Wg", [P, 2, XW])
        Wl = sb("Wl", [P, 2, D])
        identf = sb("identf", [P, P])
        identb = sb("identb", [P, P], bf16)
        onesb = sb("onesb", [P, 2], bf16)
        onesf = sb("onesf", [P, P])
        sel = sb("sel", [3 * H, H, P], bf16)
        nbig = sb("nbig", [P, G, P], bf16)
        iota16 = sb("iota16", [P, T2], f16)
        iotaf = sb("iotaf", [P, P])
        pidx_i = sb("pidx_i", [P, 1], i32)
        pidx = sb("pidx", [P, 1])
        idx1 = sb("idx1", [P, T1 + 2 * G], i16)
        lo1 = sb("lo1", [P, T1])
        tile1 = sb("tile1", [P, T1], i32)
        idx2 = [sb(f"idx2{d}", [P, T2 + 2 * G], i16) for d in (0, 1)]
        lo2 = [sb(f"lo2{d}", [P, T2 + 2 * G]) for d in (0, 1)]
        maps = sb("maps", [P, T2], i32)
        tile2 = [maps[64 * d:64 * d + 1, :] for d in (0, 1)]
        rel2 = [maps[64 * d + 32:64 * d + 33, :] for d in (0, 1)]
        M = sb("M", [NL, NT, H])
        n0, n1 = (sb(f"n{k}", [NL, NT, H]) for k in range(2))
        stat = sb("stat", [NL, NT, 4])
        ADC = sb("ADC", [NL, NT, 2 * H])
        used = sb("used", [P, 2], i32)
        arena = sb("arena", [P, ARENA])
        taken_words = [0]

        def place(words, at=None):
            if at is not None:
                taken_words[0] = at
            taken_words[0] += words
            assert taken_words[0] <= ARENA, taken_words[0]
            return arena[:, taken_words[0] - words:taken_words[0]]

        idxc = sb("idxc", [P, 8], i32)
        zrow = sb("zrow", [1, HW])
        row = place(8 * D, 0)[0:1, :].rearrange("p (k f) -> p k f", k=8)
        prod = place(2 * D).rearrange("p (c f) -> p c f", c=2)
        stab = place(NT * 3 * H // 2)[0:NL, :].bitcast(bf16).rearrange("p (t k) -> p t k", t=NT)
        xs = place(D)[0:NL, :]
        xT = place(2 * NL)
        sring = place(8 * 3 * H // 2, 4200).bitcast(bf16).rearrange("p (u k) -> p u k", u=8)
        asT = place(2 * P // 2)[0:3 * H, :].bitcast(bf16).rearrange("p (u e) -> p u e", u=2)
        mx = place(8 * H)[0:NL, :].rearrange("p (u h) -> p u h", u=8)
        noh = place(4 * 63).bitcast(bf16).rearrange("p (u n) -> p u n", u=4)[:, :, 0:NL]
        ring = place(8 * HW, 0).rearrange("p (u f) -> p u f", u=8)
        scaled = place(G * HW).rearrange("p (u f) -> p u f", u=G)
        oh = place(4 * G * NL).rearrange("p (u n) -> p u n", u=4 * G)
        ohT = place(G * P)[0:NL, :].rearrange("p (u e) -> p u e", u=G)
        small = place(3 * G * H).rearrange("p (k m) -> p k m", k=3)
        low = place(NT * D // 2, 0)[0:NL, :].bitcast(bf16).rearrange("p (t f) -> p t f", t=NT)
        xring = place(8 * 3 * D // 2, 0).bitcast(bf16).rearrange("p (u f) -> p u f", u=8)
        att = place(G * 2 * NL).rearrange("p (u k) -> p u k", u=G)
        ohb = place(8 * 63).bitcast(bf16).rearrange("p (u n) -> p u n", u=8)[:, :, 0:NL]
        PS = ctx.enter_context(nc.psum_tensor("PS", [P, 8, 512], f32))

        at = [0]

        def cut(words):
            at[0] += words
            assert at[0] <= 2 * R * 2 * D
            return WR[:, at[0] - words:at[0]]

        own_i, oth_i, typ_i = (cut(C0).bitcast(i32) for _ in range(3))
        hi, lo, Av, Bv, t0, t1, t2, pos, jf, sf = (cut(T1) for _ in range(10))
        rowtot, offs, r0, r1 = (cut(NT) for _ in range(4))
        c0, c1, c2, c3 = (cut(1) for _ in range(4))
        cmp16 = cut(T2 // 2).bitcast(f16)
        dmap = cut(T1)
        A1, B1, typ1 = (cut(T1) for _ in range(3))
        masks = cut(R * T1 // 2).bitcast(f16).rearrange("p (t j) -> p t j", t=R)
        cntj = cut(4 * R)
        dT = cut(4 * NT)
        cnt, end2, shift, s0, s1 = (cut(R) for _ in range(5))
        shiftb = cut(P)
        ohj = cut(4 * (T2 // 2)).bitcast(f16).rearrange("p (u j) -> p u j", u=4)
        lab = cut(4 * P).bitcast(f16).rearrange("p (u k s) -> p u k s", u=4, k=2)
        q0, q1 = cut(T2), cut(T2)
        iota_i = q0.bitcast(i32)
        onesw = cut(T1)
        trif, triif = cut(P), cut(P)
        tri16, ones16, zero16 = (cut(P // 2).bitcast(f16) for _ in range(3))
        parts = ACC[1][:, :, 0:D].bitcast(bf16)

        gate = sem("gate")
        filled = sem("filled")
        made = sem("made")
        x_in, w_in, rows_in, wr_in = sem("x_in"), sem("w_in"), sem("rows_in"), sem("wr_in")
        edges_in = [sem(f"edges_in{d}") for d in (0, 1)]
        vs = sem("vs")
        spread = sem("spread")
        wg_ready = sem("wg_ready")
        act_lin, pe_lin = sem("act_lin"), sem("pe_lin")
        sort_in, sort_out = sem("sort_in"), sem("sort_out")
        perm_in, perm_out = sem("perm_in"), sem("perm_out")
        sort_done = sem("sort_done")
        tab_ready = sem("tab_ready")
        h_out, s_out, x_out = sem("h_out"), sem("s_out"), sem("x_out")
        gath = [sem(f"gath{u}") for u in range(8)]
        idx_ready, slot_free = sem("idx_ready"), sem("slot_free")
        noh_ready, turned, ast_ready = sem("noh_ready"), sem("turned"), sem("ast_ready")
        v_done, max_taken = sem("v_done"), sem("max_taken")
        oh_ready, oht_ps, oht_ready = sem("oh_ready"), sem("oht_ps"), sem("oht_ready")
        adc_done, z_ready, p_ready = sem("adc_done"), sem("z_ready"), sem("p_ready")
        hp_ready, agg_done, acc_taken = sem("hp_ready"), sem("agg_done"), sem("acc_taken")
        shift_ready, self_exp = sem("shift_ready"), sem("self_exp")
        gath2 = [[sem(f"gath2{d}{u}") for u in range(8)] for d in (0, 1)]
        idx2_ready = [sem(f"idx2_ready{d}") for d in (0, 1)]
        roh_ready = [sem(f"roh_ready{d}") for d in (0, 1)]
        at_ps = [sem(f"at_ps{d}") for d in (0, 1)]
        at_ready = [sem(f"at_ready{d}") for d in (0, 1)]
        y_done = [sem(f"y_done{d}") for d in (0, 1)]
        y_taken = [sem(f"y_taken{d}") for d in (0, 1)]
        over = [sem(f"over{d}") for d in (0, 1)]
        ln_act, ln_in = sem("ln_act"), sem("ln_in")
        fin_act, fin_ps, fin_taken = sem("fin_act"), sem("fin_ps"), sem("fin_taken")
        out_ready, out_done = sem("out_ready"), sem("out_done")

        block = ctx.enter_context(nc.Block())

        def loads(eng, which, row_, top):
            _, values = nc.values_load_multi_w_load_instructions(
                row_, engines=[which], min_val=0, max_val=top,
                skip_runtime_bounds_check_because="VectorE has bounded them")
            return values

        def node_rows(t):
            return t.rearrange("(t p) f -> p t f", p=NL)

        WV = WR[:, :].rearrange("p (d r c o) -> p d r c o", d=2, r=R, c=2)
        dbg = a.get("dbg", {})
        loc = locals()

        @block.sync
        def _(sp):
            for k, name in enumerate(("L0_gnn_att_src", "L0_gnn_att_dst", "L0_gnn_bias", "L0_gnn_ln_gamma", "L0_gnn_ln_beta",
                                      "L1_gnn_forward_bias", "L1_gnn_backward_bias", "L1_gnn_self_bias")):
                v = a[name].rearrange("h c -> (h c)") if k < 2 else a[name]
                sp.dma_start(row[:, k, :], v.rearrange("(a n) -> a n", a=1)).then_inc(rows_in, 16)
            sp.dma_start(Wg[:, :, 0:D], a["L0_gnn_W"].rearrange("(c p) o -> p c o", p=P)).then_inc(w_in, 16)
            sp.dma_start(X[:, :, :], node_rows(a["x"])).then_inc(x_in, 16)
            sp.dma_start(Wl[:, :, :], a["L1_gnn_loop_weight"].rearrange("(c p) o -> p c o", p=P)).then_inc(w_in, 16)
            for d, names in enumerate((("dst", "src"), ("src", "dst"))):
                sp.wait_ge(made, d + 1)
                for buf, name in zip((own_i, oth_i, typ_i), (*names, "edge_type_16")):
                    sp.dma_start(buf[0:FULL, :], a[name][0:FULL * C0].rearrange("(p c) -> p c", c=C0)).then_inc(edges_in[d], 16)
                    sp.dma_start(buf[FULL:FULL + 1, 0:REST],
                                 a[name][FULL * C0:E].rearrange("(p c) -> p c", p=1)).then_inc(edges_in[d], 16)
                if d == 0:
                    sp.wait_ge(act_lin, 3 * NT)
                    sp.dma_start(node_rows(h_table[0:N, :]), Hn[:, :, 0:HW]).then_inc(h_out, 16)
                    sp.wait_ge(tab_ready, 1)
                    sp.dma_start(node_rows(s_table[0:N, :]), stab).then_inc(s_out, 16)
                    sp.dma_start(s_table[N:N + 1, :], zrow[0:1, 0:3 * H // 2].bitcast(bf16)).then_inc(s_out, 16)
                    sp.dma_start(h_table[N:N + 1, :], zrow[:, :]).then_inc(h_out, 16)
            sp.wait_ge(sort_done, 2)
            for d, name in enumerate(("L1_gnn_Wf", "L1_gnn_Wb")):
                for c in range(2):
                    sp.dma_start(WV[:, d, :, c, :], a[name][:, c * P:(c + 1) * P, :].rearrange("r p o -> p r o")).then_inc(wr_in, 16)
            sp.wait_ge(tab_ready, 2)
            sp.dma_start(node_rows(x_table[:, 0:2 * D]), parts).then_inc(x_out, 16)
            sp.dma_start(node_rows(x_table[:, 2 * D:3 * D]), low).then_inc(x_out, 16)
            sp.wait_ge(out_ready, 1)
            sp.dma_start(node_rows(out), ACC[0][:, :, 0:D]).then_inc(out_done, 16)
            for f, dst in dbg.values():
                sp.dma_start(dst, f(loc)).then_inc(out_done, 16)
            sp.wait_ge(out_done, 16 + 16 * len(dbg))

        @block.gpsimd
        def _(pool):
            pool.iota(iota_i[:, :], [[1, T2]], base=0, channel_multiplier=0).then_inc(filled, 1)
            pool.iota(pidx_i[:, :], [[1, 1]], base=0, channel_multiplier=1).then_inc(filled, 1)
            pool.memset(identf[:, :], 0.0).then_inc(filled, 1)
            pool.memset(identb[:, :], 0.0).then_inc(filled, 1)
            pool.memset(trif[:, :], 1.0).then_inc(filled, 1)
            pool.memset(triif[:, :], 1.0).then_inc(filled, 1)
            pool.memset(sel[:, :, :], 0.0).then_inc(filled, 1)
            pool.memset(nbig[:, :, :], 0.0).then_inc(filled, 1)
            pool.wait_ge(filled, 8)
            for m in (identf, identb):
                pool.affine_select(out=m[:, :], in_=m[:, :], compare_op=ALU.not_equal, fill=1.0, base=0,
                                   pattern=[[-1, P]], channel_multiplier=1).then_inc(filled, 1)
            pool.affine_select(out=trif[:, :], in_=trif[:, :], compare_op=ALU.is_gt, fill=0.0, base=0,
                               pattern=[[1, P]], channel_multiplier=-1).then_inc(filled, 1)
            pool.affine_select(out=triif[:, :], in_=triif[:, :], compare_op=ALU.is_ge, fill=0.0, base=0,
                               pattern=[[1, P]], channel_multiplier=-1).then_inc(filled, 1)
            pool.affine_select(out=nbig[:, :, :], in_=nbig[:, :, :], compare_op=ALU.not_equal, fill=ABSENT, base=0,
                               pattern=[[0, G], [-1, P]], channel_multiplier=1).then_inc(filled, 1)
            for m in range(3):
                pool.affine_select(out=sel[:, :, :], in_=sel[:, :, :], compare_op=ALU.not_equal, fill=1.0, base=-H * m,
                                   pattern=[[-1, H], [0, P]], channel_multiplier=1).then_inc(filled, 1)
                pool.wait_ge(filled, 14 + m)

            for phase in range(2):
                pool.wait_ge(h_out if phase else s_out, 32)
                first = phase * T1
                with pool.Fori(0, T1 // 8) as i:
                    for u in range(8):
                        if u % G == 0:
                            pool.wait_ge(idx_ready, first // G + 2 * phase + 2 * i + u // G + 1)
                        pool.wait_ge(slot_free if phase else turned, 8 * i + u + 1)
                        pool.sem_inc(gate, 1)
                        dst, table = (ring, h_table) if phase else (sring, s_table)
                        pool.indirect_dma_start(out=dst[:, u, :], out_offset=None, in_=table,
                                                in_offset=bass.IndirectOffsetOnAxis(ap=idxc[:, u:u + 1], axis=0)
                                                ).then_inc(gath[u], 16)
            pool.wait_ge(x_out, 32)
            for d in (0, 1):
                if d:
                    pool.wait_ge(over[0], 3)
                limit = pool.value_load(used[0:1, d:d + 1], min_val=1, max_val=T2)
                with pool.Fori(0, T2 // 8) as i:
                    with pool.If(i * 8 < limit):
                        for u in range(8):
                            if u % G == 0:
                                pool.wait_ge(idx2_ready[d], 2 * i + u // G + 1)
                            pool.wait_ge(at_ps[d], 8 * i + u + 1)
                            pool.sem_inc(gate, 1)
                            pool.indirect_dma_start(out=xring[:, u, :], out_offset=None, in_=x_table,
                                                    in_offset=bass.IndirectOffsetOnAxis(ap=idxc[:, u:u + 1], axis=0)
                                                    ).then_inc(gath2[d][u], 16)

        @block.scalar
        def _(act):
            act.wait_ge(x_in, 16)
            with act.Fori(0, NT) as t:
                act.activation(xs, X[:, ds(t, 1), :].rearrange("p a f -> p (a f)"), ACT.Copy).then_inc(act_lin, 1)
                act.wait_ge(pe_lin, 2 * t + 1)
                act.activation(xT, PS[:, 0, 0:2 * NL], ACT.Copy).then_inc(act_lin, 1)
                act.wait_ge(pe_lin, 2 * t + 2)
                act.sem_inc(gate, 1)
                act.activation(Hn[:, ds(t, 1), :].rearrange("p a f -> p (a f)"), PS[0:NL, 1, 0:XW], ACT.Copy).then_inc(act_lin, 1)

            def indices(idx, ready, group, half):
                act.activation(idxc[:, half * G:(half + 1) * G], idx[:, ds(group * G, G)], ACT.Copy).then_inc(ready, 1)

            def gathers_done(sems, times, half):
                for u in range(half * G, (half + 1) * G):
                    act.wait_ge(sems[u], 16 * times)
                act.sem_inc(gate, 1)

            act.wait_ge(sort_done, 1)
            indices(idx1, idx_ready, 0, 0)
            indices(idx1, idx_ready, 1, 1)
            with act.Fori(0, T1 // 8) as i:
                for u in range(8):
                    act.wait_ge(turned, 8 * i + u + 9)
                    act.wait_ge(v_done, 8 * i + u + 1)
                    act.activation(asT[:, u % 2, :], PS[0:3 * H, 4 + u % 2, 0:P // 2].bitcast(bf16), ACT.Copy).then_inc(ast_ready, 1)
                    if u % G == G - 1:
                        gathers_done(gath, i + 1, u // G)
                        indices(idx1, idx_ready, 2 * i + 2 + u // G, u // G)
            act.wait_ge(shift_ready, 1)
            act.activation(n1[:, :, :], n0[:, :, :], ACT.Exp).then_inc(self_exp, 1)
            act.wait_ge(idx_ready, T1 // G + 2)
            indices(idx1, idx_ready, 0, 0)
            indices(idx1, idx_ready, 1, 1)

            def turned_onehots(g, q):
                act.wait_ge(oht_ps, g + 1)
                act.wait_ge(adc_done, G * g + G)
                act.activation(ohT, PS[0:NL, q % 2, :].rearrange("p (u e) -> p u e", u=G), ACT.Copy).then_inc(oht_ready, 1)

            def exps(i, q, last):
                g = 4 * i + q
                act.wait_ge(z_ready, g + 1)
                act.wait_ge(agg_done, G * g + G)
                act.activation(scaled[:, :, D:HW], small[:, 2, :].rearrange("p (u h) -> p u h", u=G), ACT.Exp).then_inc(p_ready, 1)
                gathers_done(gath, T1 // 8 + 2 * i + q // 2 + 1, q % 2)
                indices(idx1, idx_ready, g + 2, q % 2)
                if not last:
                    turned_onehots(g + 1, q + 1)

            turned_onehots(0, 0)
            with act.Fori(0, T1 // 16 - 1) as i:
                for q in range(4):
                    exps(i, q, False)
            for q in range(4):
                exps(T1 // 16 - 1, q, q == 3)
            for k in range(2):
                act.wait_ge(ln_in, k + 1)
                act.activation(stat[:, :, 3], stat[:, :, 2], ACT.Sqrt).then_inc(ln_act, 1)
            for d in (0, 1):
                if d == 0:
                    act.wait_ge(idx_ready, 2 * (T1 // G) + 4)
                else:
                    act.wait_ge(over[0], 3)
                indices(idx2[d], idx2_ready[d], 0, 0)
                indices(idx2[d], idx2_ready[d], 1, 1)
                limit = act.value_load(used[0:1, d:d + 1], min_val=1, max_val=T2)
                with act.Fori(0, T2 // 8) as i:
                    with act.If(i * 8 < limit):
                        for g in range(2):
                            for b in range(2):
                                n = 8 * i + G * g + 2 * b
                                act.wait_ge(at_ps[d], n + 2 + 8)
                                act.wait_ge(y_done[d], n + 2)
                                act.activation(att[:, 2 * b:2 * b + 2, :],
                                               PS[:, 2 * g + b, :].rearrange("p (u k) -> p u k", u=2)[:, :, 0:2 * NL],
                                               ACT.Copy).then_inc(at_ready[d], 2)
                            gathers_done(gath2[d], i + 1, g)
                            indices(idx2[d], idx2_ready[d], 2 * i + 2 + g, g)
                act.drain().then_inc(over[d], 1)
            act.wait_ge(over[1], 3)
            with act.Fori(0, NT) as t:
                act.activation(xs, X[:, ds(t, 1), :].rearrange("p a f -> p (a f)"), ACT.Copy).then_inc(fin_act, 1)
                act.wait_ge(fin_ps, 2 * t + 1)
                act.activation(xT, PS[:, 0, 0:2 * NL], ACT.Copy).then_inc(fin_act, 1)
                act.wait_ge(fin_ps, 2 * t + 2)
            act.wait_ge(ln_in, 3)
            act.activation(stat[:, :, 3], stat[:, :, 2], ACT.Sqrt).then_inc(ln_act, 1)

        @block.tensor
        def _(pe):
            def mm(*args, **kw):
                return pe.matmul(*args, **kw)

            pe.wait_ge(made, 1)
            pe.wait_ge(rows_in, 128)
            for k in range(4):
                for m in range(2):
                    last = mm(PS[:, 2 + k, m * D:(m + 1) * D], onesf[0:1, :], row[0:1, 2 * k + m, :], start=True, stop=True)
            last.then_inc(spread, 1)
            pe.wait_ge(wg_ready, 1)
            with pe.Fori(0, NT) as t:
                pe.wait_ge(act_lin, 3 * t + 1)
                for c in range(2):
                    last = pe.transpose(PS[:, 0, c * NL:(c + 1) * NL], xs[:, c * P:(c + 1) * P], identf[0:NL, 0:NL])
                last.then_inc(pe_lin, 1)
                pe.wait_ge(act_lin, 3 * t + 2)
                for c in range(2):
                    last = mm(PS[0:NL, 1, 0:XW], xT[:, c * NL:(c + 1) * NL], Wg[:, c, :], start=c == 0, stop=c == 1)
                last.then_inc(pe_lin, 1)
            pe.wait_ge(act_lin, 3 * NT)

            si, so = Steps(sort_in), Steps(sort_out)
            pi, po = Steps(perm_in), Steps(perm_out)

            def permute(cols, width):
                parts = width // T1 if width == T1 else 2
                w = width // parts
                pe.wait_ge(sort_in, si.step())
                for k in range(2):
                    for h in range(parts):
                        last = mm(PS[:, 4 + k * parts + h, 0:w], zero16[:, :], iota16[:, 0:w], start=True, stop=False)
                last.then_inc(perm_out, 4)
                po.base += 4
                with pe.Fori(0, cols // 4) as i:
                    for u in range(4):
                        pe.wait_ge(perm_in, pi.base + 4 * i + u + 1)
                        for k in range(2):
                            for h in range(parts):
                                last = mm(PS[:, 4 + k * parts + h, 0:w], lab[:, u, k, :], ohj[:, u, h * w:(h + 1) * w], start=False, stop=False)
                        last.then_inc(perm_out, 1)
                pi.base += cols
                for k in range(2):
                    for h in range(parts):
                        last = mm(PS[:, 4 + k * parts + h, 0:w], zero16[:, :], iota16[:, 0:w], start=False, stop=True)
                last.then_inc(perm_out, 1)

            for d in (0, 1):
                pe.wait_ge(sort_in, si.step())
                mm(PS[:, 2, 0:NT], onesf[:, :], rowtot, start=True, stop=True)
                mm(PS[:, 2, 32:32 + NT], trif[:, :], rowtot, start=True, stop=True)
                mm(PS[0:NT, 2, 64:65], rowtot, onesf[:, 0:1], start=True, stop=True).then_inc(sort_out, 1)
                pe.wait_ge(sort_in, si.step())
                mm(PS[0:NT, 2, 65:66], triif[0:NT, 0:NT], c1[0:NT, :], start=True, stop=True).then_inc(sort_out, 1)
                pe.wait_ge(sort_in, si.step())
                mm(PS[:, 3, 0:T1], ones16[0:NT, :], cmp16[0:NT, 0:T1], start=True, stop=True).then_inc(sort_out, 1)
                permute(C0, T1)
                pe.wait_ge(sort_in, si.step())
                with pe.Fori(0, R) as t:
                    for k in range(4):
                        last = mm(PS[0:T1 // 4, 2, ds(t + 16 * k, 1)], masks[:, ds(t, 1), k * (T1 // 4):(k + 1) * (T1 // 4)].rearrange("p a j -> p (a j)"),
                                  ones16[:, 0:1], start=True, stop=True)
                last = mm(PS[0:1, 2, 64:65], ones16[:, 0:1], ones16[:, 0:1], start=True, stop=True)
                last.then_inc(sort_out, 1)
                pe.wait_ge(sort_in, si.step())
                for k in range(4):
                    last = mm(PS[0:NT, 2, 128:128 + R], dT[0:T1 // 4, k * NT:(k + 1) * NT], cntj[0:T1 // 4, k * R:(k + 1) * R], start=k == 0, stop=k == 3)
                last.then_inc(sort_out, 1)
                pe.wait_ge(sort_in, si.step())
                mm(PS[0:NT, 2, 160:160 + R], trif[0:NT, 0:NT], cnt[0:NT, :], start=True, stop=True)
                mm(PS[0:NT, 2, 176:177], trif[0:NT, 0:NT], end2[0:NT, R - 1:R], start=True, stop=True).then_inc(sort_out, 1)
                for t in range(R):
                    pe.wait_ge(sort_in, si.step())
                    for h in range(2):
                        last = mm(PS[:, h, 0:T2 // 2], ones16[0:NT, :], cmp16[0:NT, h * (T2 // 2):(h + 1) * (T2 // 2)], start=t == 0, stop=t == R - 1)
                        if t == R - 1:
                            last = mm(PS[:, 4 + h, 0:T2 // 2], ones16[0:NT, :], cmp16[0:NT, h * (T2 // 2):(h + 1) * (T2 // 2)], start=True, stop=True)
                    last.then_inc(sort_out, 1)
                a0 = si.base
                with pe.Fori(0, R) as t:
                    pe.wait_ge(sort_in, a0 + t + 1)
                    mm(PS[:, 2, 0:T1], tri16[:, :], masks[:, ds(t, 1), :].rearrange("p a j -> p (a j)"), start=True, stop=False)
                    mm(PS[:, 2, 0:T1], shiftb[0:NT, :], dmap[0:NT, :], start=False, stop=True)
                    mm(PS[:, 3, 0:T1], ones16[:, :], masks[:, ds(t, 1), :].rearrange("p a j -> p (a j)"), start=True, stop=True).then_inc(sort_out, 1)
                si.base += R
                permute(T1, T2)

            pe.wait_ge(sort_done, 2)
            pe.sem_inc(v_done, 2)
            pe.sem_inc(turned, 8)

            def turn(i, u):
                pe.wait_ge(gath[u], 16 * (i + 1))
                if not (isinstance(i, int) and 8 * i + u < 2):
                    pe.wait_ge(ast_ready, 8 * i + u - 1)
                pe.transpose(PS[0:3 * H, 4 + u % 2, 0:P // 2].bitcast(bf16), sring[:, u, :], identb[:, :]).then_inc(turned, 1)

            def values(i, u):
                pe.wait_ge(noh_ready, 8 * i + u + 1)
                pe.wait_ge(max_taken, 8 * i + u + 1)
                for b in range(2):
                    mm(PS[0:NL, (u % 2) * 2 + b, :], noh[:, u % 4, :], nbig[:, :, :].rearrange("p a b -> p (a b)"), start=True, stop=False)
                pe.wait_ge(ast_ready, 8 * i + u + 1)
                for h in range(H):
                    last = mm(PS[0:NL, (u % 2) * 2 + h // 4, (h % 4) * P:(h % 4 + 1) * P], sel[:, h, 0:NL], asT[:, u % 2, :],
                              start=False, stop=h % 4 == 3)
                last.then_inc(v_done, 1)

            turn(0, 0)
            for u in range(8):
                if u < 7:
                    turn(0, u + 1)
                else:
                    turn(1, 0)
                values(0, u)
            with pe.Fori(1, T1 // 8 - 1) as i:
                for u in range(8):
                    if u < 7:
                        turn(i, u + 1)
                    else:
                        turn(i + 1, 0)
                    values(i, u)
            for u in range(8):
                if u < 7:
                    turn(T1 // 8 - 1, u + 1)
                values(T1 // 8 - 1, u)

            pe.wait_ge(shift_ready, 1)
            pe.sem_inc(adc_done, G)
            pe.sem_inc(agg_done, G)

            def to_edges(g, q):
                tiles = loads(pe, mybir.EngineType.PE, tile1[0:1, ds(G * g, G)], NT - 1)
                pe.wait_ge(oh_ready, G * g + G)
                for u in range(G):
                    last = pe.transpose(PS[0:NL, q % 2, u * P:(u + 1) * P], oh[:, (G * q + u) % (4 * G), :], identf[:, :])
                last.then_inc(oht_ps, 1)
                pe.wait_ge(oht_ready, g + 1)
                for u in range(G):
                    mm(PS[:, 2 + q % 2, u * 2 * H:(u + 1) * 2 * H], ohT[:, u, :], ADC[:, ds(tiles[u], 1), :].rearrange("p a k -> p (a k)"),
                       start=True, stop=True).then_inc(adc_done, 1)

            def sums(i, q, last):
                g = 4 * i + q
                if not last:
                    to_edges(g + 1, q + 1)
                for u in range(G):
                    pe.wait_ge(hp_ready, G * g + u + 1)
                    pe.wait_ge(acc_taken, G * g + u + 1)
                    mm(PS[0:NL, 4 + u, 0:HW], oh[:, G * q + u, :], scaled[:, u, :], start=True, stop=True).then_inc(agg_done, 1)

            to_edges(0, 0)
            with pe.Fori(0, T1 // 16 - 1) as i:
                for q in range(4):
                    sums(i, q, False)
            for q in range(4):
                sums(T1 // 16 - 1, q, q == 3)

            pe.wait_ge(wr_in, 64)
            for d in (0, 1):
                if d:
                    pe.wait_ge(over[0], 3)
                else:
                    pe.wait_ge(x_out, 32)
                pe.sem_inc(y_done[d], G)
                pe.sem_inc(at_ps[d], 8)
                limit = pe.value_load(used[0:1, d:d + 1], min_val=1, max_val=T2)
                with pe.Fori(0, T2 // 8) as i:
                    with pe.If(i * 8 < limit):
                        for g in range(2):
                            rels = loads(pe, mybir.EngineType.PE, rel2[d][0:1, ds(8 * i + G * g, G)], R - 1)
                            for u in range(G):
                                n = 8 * i + G * g + u
                                b = g * 2 + u // 2
                                pe.wait_ge(gath2[d][G * g + u], 16 * (i + 1))
                                pe.wait_ge(roh_ready[d], n + 1)
                                for c in range(2):
                                    for k in range(3):
                                        last = mm(PS[:, b, (u % 2) * 256 + c * NL:(u % 2) * 256 + (c + 1) * NL],
                                                  xring[:, G * g + u, k * D + c * P:k * D + (c + 1) * P], ohb[:, G * g + u, :], start=k == 0, stop=k == 2)
                                last.then_inc(at_ps[d], 1)
                            for u in range(G):
                                n = 8 * i + G * g + u
                                pe.wait_ge(at_ready[d], n + 1)
                                pe.wait_ge(y_taken[d], n + 1)
                                for c in range(2):
                                    mm(PS[0:NL, 4 + u, 0:D], att[:, u, c * NL:(c + 1) * NL], WV[:, d, ds(rels[u], 1), c, :].rearrange("p a o -> p (a o)"), start=c == 0, stop=c == 1)
                                mm(PS[0:NL, 4 + u, D:D + 1], ohb[:, G * g + u, :], onesb[:, 0:1], start=True, stop=True).then_inc(y_done[d], 1)
                pe.drain().then_inc(over[d], 1)
            with pe.Fori(0, NT) as t:
                pe.wait_ge(fin_act, 2 * t + 1)
                for c in range(2):
                    last = pe.transpose(PS[:, 0, c * NL:(c + 1) * NL], xs[:, c * P:(c + 1) * P], identf[0:NL, 0:NL])
                last.then_inc(fin_ps, 1)
                pe.wait_ge(fin_act, 2 * t + 2)
                pe.wait_ge(fin_taken, t + 1)
                for c in range(2):
                    last = mm(PS[0:NL, 1, 0:D], xT[:, c * NL:(c + 1) * NL], Wl[:, c, :], start=c == 0, stop=c == 1)
                last.then_inc(fin_ps, 1)

        @block.vector
        def _(dve):
            S = Steps(vs)

            def v(ins):
                ins.then_inc(vs, 1)
                dve.wait_ge(vs, S.step())

            def ts(out, in_, s1, op0, s2=None, op1=ALU.bypass, **kw):
                return dve.tensor_scalar(out, in_, s1, s2, op0, op1, **kw)

            def stt(out, in0, s, in1, op0, op1):
                return dve.scalar_tensor_tensor(out=out, in0=in0, scalar=s, in1=in1, op0=op0, op1=op1)

            cp, tt = dve.tensor_copy, dve.tensor_tensor

            v(dve.memset(ones16[:, :], 1.0))
            v(dve.memset(onesf[:, :], 1.0))
            v(dve.memset(onesw[:, :], 1.0))
            v(dve.memset(onesb[:, :], 1.0))
            v(dve.memset(zrow[:, :], 0.0))
            v(dve.memset(zero16[:, :], 0.0))
            for idx, w in ((idx1, T1), (idx2[0], T2), (idx2[1], T2)):
                v(dve.memset(idx[:, w:w + 2 * G], 0))
            for lo_ in lo2:
                v(dve.memset(lo_[:, T2:T2 + 2 * G], 0.0))
            v(dve.memset(own_i, 4000))
            v(dve.memset(oth_i, 0))
            v(dve.memset(typ_i, 0))
            dve.wait_ge(filled, 16)
            v(cp(iota16[:, :], iota_i[:, :]))
            v(cp(iotaf[:, :], iota_i[:, 0:P]))
            v(cp(pidx[:, :], pidx_i[:, :]))
            v(cp(tri16[:, :], trif[:, :]))
            dve.sem_inc(made, 1)
            dve.wait_ge(spread, 1)
            v(cp(bc[:, :, :], PS[:, 2:6, :].rearrange("p b (k f) -> p (b k) f", k=2)))
            dve.wait_ge(w_in, 32)
            for k in range(2):
                v(tt(prod, Wg[:, :, 0:D],
                     bc[:, k:k + 1, :].broadcast_to([P, 2, D]), ALU.mult))
                v(dve.reduce_sum(Wg[:, :, D + k * H:D + (k + 1) * H],
                                 prod.rearrange("p c (h f) -> p c h f", h=H), AX.X))
            dve.sem_inc(wg_ready, 1)

            so = Steps(sort_out)
            perm = [0, 0]

            def ask():
                dve.sem_inc(sort_in, 1)
                dve.wait_ge(sort_out, so.step())

            def split(width, p):
                v(cp(t0[:, 0:width].bitcast(i32), p))
                v(ts(t1[:, 0:width].bitcast(i32), t0[:, 0:width].bitcast(i32), 7, ALU.logical_shift_right))
                v(ts(t2[:, 0:width].bitcast(i32), t0[:, 0:width].bitcast(i32), P - 1, ALU.bitwise_and))
                v(cp(jf[:, 0:width], t1[:, 0:width].bitcast(i32)))
                v(cp(sf[:, 0:width], t2[:, 0:width].bitcast(i32)))

            def permute(cols, width, va, vb):
                dve.sem_inc(sort_in, 1)
                with dve.Fori(0, cols // 4) as i:
                    for u in range(4):
                        c = i * 4 + u
                        dve.wait_ge(perm_out, perm[1] + 4 * i + u + 1)
                        ts(ohj[:, u, 0:width], iota16[:, 0:width], jf[:, ds(c, 1)], ALU.is_equal)
                        ts(lab[:, u, 0, :], iota16[:, 0:P], sf[:, ds(c, 1)], ALU.is_equal, va[:, ds(c, 1)], ALU.mult)
                        ts(lab[:, u, 1, :], iota16[:, 0:P], sf[:, ds(c, 1)], ALU.is_equal, vb[:, ds(c, 1)], ALU.mult).then_inc(perm_in, 1)
                perm[1] += 4 + cols + 1
                dve.wait_ge(perm_out, perm[1])

            def slots_of(dst, src):
                v(cp(dst.bitcast(i32), src))
                v(ts(dst.bitcast(i32), dst.bitcast(i32), P - 1, ALU.add))
                v(ts(dst.bitcast(i32), dst.bitcast(i32), 7, ALU.logical_shift_right))

            for d in (0, 1):
                E0 = slice(0, C0)
                dve.wait_ge(edges_in[d], 96)
                v(cp(hi[:, E0], own_i))
                v(cp(Av[:, E0], oth_i))
                v(cp(Bv[:, E0], typ_i))
                v(ts(t0[:, E0], hi[:, E0], 1.0 / NL, ALU.mult, 0.5 / NL - 0.5, ALU.add))
                v(cp(jf[:, E0].bitcast(i32), t0[:, E0]))
                v(cp(t0[:, E0], jf[:, E0].bitcast(i32)))
                v(stt(t1[:, E0], t0[:, E0], -float(NL), hi[:, E0], ALU.mult, ALU.add))
                v(ts(t2[:, E0], t1[:, E0], float(NL), ALU.is_ge))
                v(ts(pos[:, E0], t1[:, E0], 0.0, ALU.is_lt))
                v(tt(t2[:, E0], t2[:, E0], pos[:, E0], ALU.subtract))
                v(tt(hi[:, E0], t0[:, E0], t2[:, E0], ALU.add))
                v(stt(lo[:, E0], t2[:, E0], -float(NL), t1[:, E0], ALU.mult, ALU.add))
                v(ts(lo[:, E0], lo[:, E0], 1.0, ALU.add, 16.0, ALU.mult))
                v(tt(Bv[:, E0], Bv[:, E0], lo[:, E0], ALU.add))
                v(ts(Av[:, E0], Av[:, E0], -float(OFF), ALU.add))
                if d == 0:
                    dve.wait_ge(edges_in[0], 96)
                with dve.Fori(0, NT) as b:
                    S.loop(b, 1)
                    v(ts(t0[:, E0], hi[:, E0], iotaf[:, ds(b, 1)], ALU.is_equal, None, ALU.add, accum_out=rowtot[:, ds(b, 1)]))
                S.end(NT)
                ask()
                slots_of(r1, PS[:, 2, 0:NT])
                v(cp(offs, r1.bitcast(i32)))
                v(ts(r1, offs, 1.0, ALU.mult))
                v(dve.tensor_tensor_scan(r0, onesf[:, 0:NT], r1, 0.0, ALU.mult, ALU.add))
                v(tt(offs, r0, r1, ALU.subtract))
                v(stt(offs, offs, float(P), PS[:, 2, 32:32 + NT], ALU.mult, ALU.add))
                v(ts(offs, offs, -1.0, ALU.add))
                slots_of(c0[0:NT, :], PS[0:NT, 2, 64:65])
                v(cp(c1[0:NT, :], c0[0:NT, :].bitcast(i32)))
                ask()
                v(cp(c2[0:NT, :], PS[0:NT, 2, 65:66]))
                v(ts(cmp16[0:NT, 0:T1], iota16[0:NT, 0:T1], c2[0:NT, :], ALU.is_ge))
                ask()
                v(ts(q0[:, 0:T1], PS[:, 3, 0:T1], float(NT - 1), ALU.min))
                if d == 0:
                    v(cp(tile1[:, :], q0[:, 0:T1]))
                v(ts(dmap[0:NT, :], q0[0:NT, 0:T1], pidx[0:NT, :], ALU.is_equal))
                v(ts(pos[:, E0], hi[:, E0], float(NT), ALU.is_ge, FAR, ALU.mult))
                with dve.Fori(0, NT) as b:
                    S.loop(b, 4)
                    v(ts(t0[:, E0], hi[:, E0], iotaf[:, ds(b, 1)], ALU.is_equal))
                    v(dve.tensor_tensor_scan(t1[:, E0], onesw[:, E0], t0[:, E0], offs[:, ds(b, 1)], ALU.mult, ALU.add))
                    v(tt(t1[:, E0], t1[:, E0], t0[:, E0], ALU.mult))
                    v(tt(pos[:, E0], pos[:, E0], t1[:, E0], ALU.add))
                S.end(NT)
                split(C0, pos[:, E0])
                permute(C0, T1, Av, Bv)
                v(cp(A1, PS[:, 4, 0:T1]))
                v(cp(B1, PS[:, 5, 0:T1]))
                v(cp(t0.bitcast(i32), B1))
                v(ts(t1.bitcast(i32), t0.bitcast(i32), 4, ALU.logical_shift_right))
                v(ts(t2.bitcast(i32), t0.bitcast(i32), R - 1, ALU.bitwise_and))
                v(cp(lo, t1.bitcast(i32)))
                v(cp(typ1, t2.bitcast(i32)))
                if d == 0:
                    v(ts(t0, lo, 0.0, ALU.is_equal, float(NONE - OFF), ALU.mult))
                    v(stt(idx1[:, 0:T1], A1, float(OFF), t0, ALU.add, ALU.add))
                    v(cp(lo1[:, :], lo))
                v(ts(t0, lo, 0.0, ALU.is_equal, 99.0, ALU.mult))
                v(tt(typ1, typ1, t0, ALU.add))
                with dve.Fori(0, R) as t:
                    S.loop(t, 1)
                    v(ts(masks[:, ds(t, 1), :].rearrange("p a j -> p (a j)"), typ1, iotaf[:, ds(t, 1)], ALU.is_equal))
                S.end(R)
                ask()
                q4 = T1 // 4
                v(cp(cntj[0:q4, :], PS[0:q4, 2, 0:4 * R]))
                for k in range(4):
                    v(ts(c3[0:q4, :], pidx[0:q4, :], float(q4 * k), ALU.add))
                    v(ts(q1[0:q4, 0:NT], r0[0:q4, :], c3[0:q4, :], ALU.is_le, None, ALU.add, accum_out=c0[0:q4, :]))
                    v(ts(c0[0:q4, :], c0[0:q4, :], float(NT - 1), ALU.min))
                    v(ts(dT[0:q4, k * NT:(k + 1) * NT], iotaf[0:q4, 0:NT], c0[0:q4, :], ALU.is_equal))
                ask()
                v(cp(cnt[0:NT, :], PS[0:NT, 2, 128:128 + R]))
                slots_of(s0[0:NT, :], cnt[0:NT, :])
                v(cp(s1[0:NT, :], s0[0:NT, :].bitcast(i32)))
                v(dve.tensor_tensor_scan(end2[0:NT, :], onesf[0:NT, 0:R], s1[0:NT, :], 0.0, ALU.mult, ALU.add))
                ask()
                v(cp(c2[0:NT, :], PS[0:NT, 2, 176:177]))
                v(ts(end2[0:NT, :], end2[0:NT, :], c2[0:NT, :], ALU.add))
                v(tt(shift[0:NT, :], end2[0:NT, :], s1[0:NT, :], ALU.subtract))
                v(stt(shift[0:NT, :], shift[0:NT, :], float(P), PS[0:NT, 2, 160:160 + R], ALU.mult, ALU.subtract))
                for t in range(R):
                    v(ts(cmp16[0:NT, :], iota16[0:NT, :], end2[0:NT, t:t + 1], ALU.is_ge))
                    ask()
                halves = lambda x: x.rearrange("p (h j) -> p h j", h=2)
                v(ts(halves(q0), PS[:, 4:6, 0:T2 // 2], float(NT - 1), ALU.min))
                v(ts(halves(q1), PS[:, 0:2, 0:T2 // 2], float(NT * R), ALU.is_lt, None, ALU.add, accum_out=c0))
                v(cp(used[:, d:d + 1], c0))
                v(ts(halves(q1), PS[:, 0:2, 0:T2 // 2], float(NT * R - 1), ALU.min))
                v(stt(q1, q0, -float(R), q1, ALU.mult, ALU.add))
                v(cp(tile2[d], q0[64 * d:64 * d + 1, :]))
                v(cp(rel2[d], q1[64 * d + 32:64 * d + 33, :]))
                v(ts(pos, typ1, float(R), ALU.is_ge, FAR, ALU.mult))
                v(dve.memset(t2[:, 0:1], 0.0))
                s_in = so.base
                with dve.Fori(0, R) as t:
                    S.loop(t, 5)
                    v(ts(shiftb[0:NT, :], onesf[0:NT, :], shift[0:NT, ds(t, 1)], ALU.mult))
                    dve.sem_inc(sort_in, 1)
                    dve.wait_ge(sort_out, s_in + t + 1)
                    v(dve.tensor_tensor_scan(t2[:, 1:T1], onesw[:, 0:T1 - 1], PS[:, 3, 0:T1 - 1], 0.0, ALU.mult, ALU.add))
                    v(tt(t0, t2, PS[:, 2, 0:T1], ALU.add))
                    v(tt(t0, t0, masks[:, ds(t, 1), :].rearrange("p a j -> p (a j)"), ALU.mult))
                    v(tt(pos, pos, t0, ALU.add))
                S.end(R)
                so.base += R
                split(T1, pos)
                permute(T1, T2, A1, B1)
                v(ts(halves(idx2[d][:, 0:T2]), PS[:, 4:6, 0:T2 // 2], float(OFF), ALU.add))
                v(cp(halves(q0).bitcast(i32), PS[:, 6:8, 0:T2 // 2]))
                v(ts(q1.bitcast(i32), q0.bitcast(i32), 4, ALU.logical_shift_right))
                v(cp(lo2[d][:, 0:T2], q1.bitcast(i32)))
                if d == 0:
                    v(dve.memset(own_i, 4000))
                    v(dve.memset(oth_i, 0))
                    v(dve.memset(typ_i, 0))
                    dve.sem_inc(made, 1)
                    dve.wait_ge(act_lin, 3 * NT)
                    src_ = Hn[:, :, D:HW]
                    v(cp(stab[:, :, 0:H], src_))
                    v(tt(n0[:, :, :], src_, stab[:, :, 0:H], ALU.subtract))
                    v(cp(stab[:, :, H:2 * H], n0[:, :, :]))
                    v(tt(n0[:, :, :], n0[:, :, :], stab[:, :, H:2 * H], ALU.subtract))
                    v(cp(stab[:, :, 2 * H:3 * H], n0[:, :, :]))
                    dve.sem_inc(tab_ready, 1)
                    v(cp(M[:, :, :], src_))
                dve.sem_inc(sort_done, 1)

            dve.sem_inc(max_taken, 2)

            def absent(n, u):
                if not isinstance(n, int) or n >= 4:
                    dve.wait_ge(v_done, n - 1)
                ts(noh[:, u % 4, :], iota16[:, 1:NL + 1], lo1[:, ds(n, 1)], ALU.not_equal).then_inc(noh_ready, 1)

            def largest(n, u):
                dve.wait_ge(v_done, n + 3)
                dve.reduce_max(mx[:, u, :], PS[0:NL, (u % 2) * 2:(u % 2) * 2 + 2, :].rearrange("p b (h e) -> p (b h) e", h=4), AX.X).then_inc(max_taken, 1)

            def keep(n, u, tile):
                dve.wait_ge(max_taken, n + 3)
                m = M[:, ds(tile, 1), :].rearrange("p a h -> p (a h)")
                v(tt(m, m, mx[:, u, :], ALU.max))

            def maxima(i, last):
                tiles = [*loads(dve, mybir.EngineType.DVE, tile1[0:1, ds(8 * i, G)], NT - 1),
                         *loads(dve, mybir.EngineType.DVE, tile1[0:1, ds(8 * i + G, G)], NT - 1)]
                for u in range(8):
                    largest(8 * i + u, u)
                    if u < 4 or not last:
                        absent(8 * i + u + 4, (u + 4) % 8)
                    if u:
                        keep(8 * i + u - 1, u - 1, tiles[u - 1])
                keep(8 * i + 7, 7, tiles[7])

            for u in range(4):
                absent(u, u)
            with dve.Fori(0, T1 // 8 - 1) as i:
                S.loop(i, 8)
                maxima(i, False)
            S.end(T1 // 8 - 1)
            maxima(T1 // 8 - 1, True)

            a_src, a_dst = Hn[:, :, D:HW], Hn[:, :, HW:XW]
            v(tt(n0[:, :, :], M[:, :, :], a_dst, ALU.add))
            v(stt(ADC[:, :, H:2 * H], n0[:, :, :], 0.2, n0[:, :, :], ALU.mult, ALU.max))
            v(cp(ADC[:, :, 0:H], a_dst))
            v(tt(n0[:, :, :], a_src, a_dst, ALU.add))
            v(stt(n0[:, :, :], n0[:, :, :], 0.2, n0[:, :, :], ALU.mult, ALU.max))
            v(tt(n0[:, :, :], n0[:, :, :], ADC[:, :, H:2 * H], ALU.subtract))
            dve.sem_inc(shift_ready, 1)
            dve.wait_ge(self_exp, 1)
            with dve.Fori(0, NT) as t:
                S.loop(t, 1)
                v(tt(ACC[0][:, ds(t, 1), 0:D].rearrange("p a (h c) -> p (a h) c", h=H), Hn[:, ds(t, 1), 0:D].rearrange("p a (h c) -> p (a h) c", h=H),
                     n1[:, ds(t, 1), :].rearrange("p a (h o) -> p (a h) o", o=1).broadcast_to([NL, H, HC]), ALU.mult))
            S.end(NT)
            v(cp(ACC[0][:, :, D:HW], n1[:, :, :]))

            dve.sem_inc(acc_taken, G)
            dve.sem_inc(slot_free, 8)

            def onehots(g, q):
                for u in range(G):
                    ts(oh[:, (G * q + u) % (4 * G), :], iota16[:, 1:NL + 1], lo1[:, ds(G * g + u, 1)], ALU.is_equal).then_inc(oh_ready, 1)

            def add_sums(g, tiles):
                for u in range(G):
                    n = G * g + u
                    dve.wait_ge(agg_done, n + G + 1)
                    dve.wait_ge(acc_taken, n + G)
                    m = ACC[0][:, ds(tiles[u], 1), :].rearrange("p a f -> p (a f)")
                    tt(m, m, PS[0:NL, 4 + u, 0:HW], ALU.add).then_inc(acc_taken, 1)

            def attend(i, q, first, last):
                g = 4 * i + q
                dve.wait_ge(adc_done, G * g + 2 * G)
                for u in range(G):
                    dve.wait_ge(gath[G * (q % 2) + u], 16 * (T1 // 8 + 2 * i + q // 2 + 1))
                adc = PS[:, 2 + q % 2, 0:2 * H * G].rearrange("p (u k) -> p u k", u=G)
                z = [small[:, k, :].rearrange("p (u h) -> p u h", u=G) for k in range(3)]
                rows = ring[:, G * (q % 2):G * (q % 2) + G, :]
                v(tt(z[0], rows[:, :, D:HW], adc[:, :, 0:H], ALU.add))
                v(stt(z[1], z[0], 0.2, z[0], ALU.mult, ALU.max))
                v(tt(z[2], z[1], adc[:, :, H:2 * H], ALU.subtract))
                dve.sem_inc(z_ready, 1)
                if not last:
                    onehots(g + 1, q + 1)
                if not first:
                    tiles = loads(dve, mybir.EngineType.DVE, tile1[0:1, ds(G * g - G, G)], NT - 1)
                dve.wait_ge(p_ready, g + 1)
                for u in range(G):
                    tt(scaled[:, u, 0:D].rearrange("p (h c) -> p h c", h=H), rows[:, u, 0:D].rearrange("p (h c) -> p h c", h=H),
                       scaled[:, u, D:HW].rearrange("p (h o) -> p h o", o=1).broadcast_to([P, H, HC]), ALU.mult).then_inc(hp_ready, 1)
                if not first:
                    add_sums(g - 1, tiles)
                dve.wait_ge(hp_ready, G * g + G)
                dve.sem_inc(slot_free, G)

            onehots(0, 0)
            for q in range(4):
                attend(0, q, q == 0, False)
            with dve.Fori(1, T1 // 16 - 1) as i:
                S.loop(i - 1, 12)
                for q in range(4):
                    attend(i, q, False, False)
            S.end(T1 // 16 - 2)
            for q in range(4):
                attend(T1 // 16 - 1, q, False, q == 3)
            add_sums(T1 // G - 1, loads(dve, mybir.EngineType.DVE, tile1[0:1, T1 - G:T1], NT - 1))
            dve.wait_ge(acc_taken, T1 + G)

            def layer_norm(src_, junk, to, gamma, k):
                mean, var = stat[:, :, 0:1], stat[:, :, 2:3]
                v(dve.reduce_sum(stat[:, :, 0], src_, AX.X))
                v(ts(stat[:, :, 0], stat[:, :, 0], 1.0 / D, ALU.mult))
                v(tt(src_, src_, mean.broadcast_to([NL, NT, D]), ALU.subtract))
                v(tt(junk, src_, src_, ALU.mult))
                v(dve.reduce_sum(stat[:, :, 1], junk, AX.X))
                v(ts(stat[:, :, 2], stat[:, :, 1], 1.0 / D, ALU.mult, LN_EPS, ALU.add))
                dve.sem_inc(ln_in, 1)
                dve.wait_ge(ln_act, k)
                v(dve.reciprocal(stat[:, :, 1], stat[:, :, 3]))
                v(tt(to, src_, stat[:, :, 1:2].broadcast_to([NL, NT, D]), ALU.mult))

            def vec(k):
                return bc[0:NL, k:k + 1, :].broadcast_to([NL, NT, D])

            o, j = ACC[0][:, :, 0:D], ACC[1][:, :, 0:D]
            v(ts(n0[:, :, :], ACC[0][:, :, D:HW], 1e-16, ALU.add))
            v(dve.reciprocal(n1[:, :, :], n0[:, :, :]))
            with dve.Fori(0, NT) as t:
                S.loop(t, 1)
                oo = ACC[0][:, ds(t, 1), 0:D].rearrange("p a (h c) -> p (a h) c", h=H)
                v(tt(oo, oo, n1[:, ds(t, 1), :].rearrange("p a (h o) -> p (a h) o", o=1).broadcast_to([NL, H, HC]), ALU.mult))
            S.end(NT)
            v(tt(o, o, vec(2), ALU.add))
            layer_norm(o, j, o, None, 1)
            v(tt(o, o, vec(3), ALU.mult))
            v(tt(o, o, vec(4), ALU.add))
            v(tt(o, o, X[:, :, :], ALU.add))
            layer_norm(o, j, X[:, :, :], None, 2)
            v(cp(parts[:, :, 0:D], X[:, :, :]))
            v(tt(o, X[:, :, :], parts[:, :, 0:D], ALU.subtract))
            v(cp(parts[:, :, D:2 * D], o))
            v(tt(o, o, parts[:, :, D:2 * D], ALU.subtract))
            v(cp(low, o))
            dve.sem_inc(tab_ready, 1)

            v(dve.memset(ACC[0][:, :, 0:D + 1], 0.0))
            dve.wait_ge(x_out, 32)
            v(dve.memset(ACC[1][:, :, 0:D + 1], 0.0))
            for d in (0, 1):
                if d:
                    dve.wait_ge(over[0], 3)
                dve.sem_inc(y_taken[d], G)

                def onehots2(n):
                    for u in range(G):
                        ts(ohb[:, n[1] + u, :], iota16[:, 1:NL + 1], lo2[d][:, ds(n[0] + u, 1)], ALU.is_equal).then_inc(roh_ready[d], 1)

                onehots2((0, 0))
                onehots2((G, G))
                limit = dve.value_load(used[0:1, d:d + 1], min_val=1, max_val=T2)
                with dve.Fori(0, T2 // 8) as i:
                    with dve.If(i * 8 < limit):
                        for g in range(2):
                            tiles = loads(dve, mybir.EngineType.DVE, tile2[d][0:1, ds(8 * i + G * g, G)], NT - 1)
                            for u in range(G):
                                n = 8 * i + G * g + u
                                dve.wait_ge(y_done[d], n + G + 1)
                                dve.wait_ge(y_taken[d], n + G)
                                m = ACC[d][:, ds(tiles[u], 1), 0:D + 1].rearrange("p a f -> p (a f)")
                                tt(m, m, PS[0:NL, 4 + u, 0:D + 1], ALU.add).then_inc(y_taken[d], 1)
                            onehots2((8 * i + 8 + G * g, G * g))
                dve.drain().then_inc(over[d], 1)
            dve.wait_ge(over[1], 3)

            for d in (0, 1):
                deg = ACC[d][:, :, D:D + 1]
                v(ts(stat[:, :, 0:1], deg, 1.0, ALU.max))
                v(dve.reciprocal(stat[:, :, 1:2], stat[:, :, 0:1]))
                v(ts(stat[:, :, 2:3], deg, 1.0, ALU.min))
                v(tt(ACC[d][:, :, 0:D], ACC[d][:, :, 0:D], stat[:, :, 1:2].broadcast_to([NL, NT, D]), ALU.mult))
                with dve.Fori(0, NT) as t:
                    S.loop(t, 1)
                    m = ACC[d][:, ds(t, 1), 0:D].rearrange("p a f -> p (a f)")
                    v(stt(m, bc[0:NL, 5 + d, :], stat[:, ds(t, 1), 2:3].rearrange("p a o -> p (a o)"), m, ALU.mult, ALU.add))
                S.end(NT)
            v(tt(o, o, j, ALU.add))
            v(tt(o, o, vec(7), ALU.add))
            v(tt(o, o, X[:, :, :], ALU.add))
            dve.sem_inc(fin_taken, 1)
            with dve.Fori(0, NT) as t:
                S.loop(t, 1)
                dve.wait_ge(fin_ps, 2 * t + 2)
                m = ACC[0][:, ds(t, 1), 0:D].rearrange("p a f -> p (a f)")
                v(stt(m, PS[0:NL, 1, 0:D], 2.0, m, ALU.mult, ALU.add))
                dve.sem_inc(fin_taken, 1)
            S.end(NT)
            layer_norm(o, j, o, None, 3)
            dve.sem_inc(out_ready, 1)


NAMES = ("x", "src", "dst", "edge_type_16", "L0_gnn_W", "L0_gnn_att_src", "L0_gnn_att_dst", "L0_gnn_bias", "L0_gnn_ln_gamma",
         "L0_gnn_ln_beta", "L1_gnn_Wf", "L1_gnn_Wb", "L1_gnn_loop_weight", "L1_gnn_forward_bias", "L1_gnn_backward_bias",
         "L1_gnn_self_bias")


def kernel(**inputs):
    import concourse.bacc as bacc
    from concourse.bass_utils import run_bass_kernel_spmd

    nc = bacc.Bacc("TRN2", target_bir_lowering=False, num_devices=1)
    arrays, aps = {}, {}
    for name in NAMES:
        arrays[name] = np.ascontiguousarray(inputs[name])
        aps[name] = nc.dram_tensor(name, arrays[name].shape, mybir.dt.from_np(arrays[name].dtype), kind="ExternalInput").ap()
    out = nc.dram_tensor("result", (N, D), f32, kind="ExternalOutput").ap()
    build_program(nc, aps, out)
    ran = run_bass_kernel_spmd(nc, [arrays], core_ids=[0])
    return ran.results[0]["result"]
```

```python
import numpy as np
import concourse.bass as bass
from concourse import mybir
from contextlib import ExitStack

ARENA = 5912
P = 128
N, D, H, R = 3125, 256, 8, 16
HC = D // H
E = 50000
NL = 112
NT = -(-N // NL)
LAST = N - (NT - 1) * NL
assert LAST < NL
C0 = 392
FULL = E // C0
REST = E - FULL * C0
T1 = 424
T2 = 840
assert T1 * P >= E + (P - 1) * NT and T2 * P >= E + (P - 1) * NT * R
assert T1 % 8 == 0 and T2 % 8 == 0
NARROW = 512
PLACE_BANKS, COLUMN_BANKS = (2, 0, 4, 6), (3, 1, 5, 7)
TURN_BANKS = (0, 6)
assert NT % 4 == 0
BLOCK = 5
assert T2 % (8 * BLOCK) == 0 and T1 <= NARROW < T2 <= 2 * NARROW
ROUNDS = (T1 // 4 - 1) // 4
TAIL = T1 // 4 - 4 * ROUNDS
HW = D + H
XW = D + 2 * H
G = 4
OFF = 1600
NONE = N
FAR = 128.0 * 1024
ABSENT = -(2.0 ** 100)
LN_EPS = 1e-5

f32, f16, bf16 = mybir.dt.float32, mybir.dt.float16, mybir.dt.bfloat16
i16, i32 = mybir.dt.int16, mybir.dt.int32
ALU = mybir.AluOpType
ACT = mybir.ActivationFunctionType
AX = mybir.AxisListType
ds = bass.ds


class Steps:

    def __init__(self, sem):
        self.sem, self.base, self.k, self.i, self.per = sem, 0, 0, None, 0

    def loop(self, i, per):
        self.i, self.per, self.k = i, per, 0

    def end(self, times):
        assert self.k == self.per, (self.k, self.per)
        self.base += self.per * times
        self.i, self.k = None, 0

    @property
    def now(self):
        if self.i is None:
            return self.base
        return self.base + self.i * self.per + self.k

    def step(self):
        if self.i is None:
            self.base += 1
        else:
            self.k += 1
        return self.now


def build_program(nc, a, out):
    ctx = ExitStack()
    with ctx:
        def sb(name, shape, dt=f32):
            return ctx.enter_context(nc.sbuf_tensor(name, shape, dt))

        def sem(name):
            return ctx.enter_context(nc.semaphore(name))

        h_table = nc.dram_tensor("h_table", (NT * NL, HW), f32).ap()
        s_table = nc.dram_tensor("s_table", (NT * NL, 3 * H), bf16).ap()
        x_table = nc.dram_tensor("x_table", (NT * NL, 3 * D), bf16).ap()

        X = sb("X", [NL, NT, D])
        ACC = [sb("ACC0", [NL, NT, HW]), sb("ACC1", [NL, NT, XW])]
        Hn = ACC[1]
        WR = sb("WR", [P, 2 * R * 2 * D])
        bc = sb("bc", [P, 6, D])
        Wg = sb("Wg", [P, 2, XW])
        identf = sb("identf", [P, P])
        identb = sb("identb", [P, P], bf16)
        onesb = sb("onesb", [P, 2], bf16)
        onesf = sb("onesf", [P, P])
        iota16 = sb("iota16", [P, T2], f16)
        iotaf = sb("iotaf", [P, P])
        pidx_i = sb("pidx_i", [P, 1], i32)
        pidx = sb("pidx", [P, 1])
        idx1 = sb("idx1", [P, T1 + 2 * G], i16)
        lo1 = sb("lo1", [P, T1 + 2 * G])
        tile1 = sb("tile1", [P, T1], i32)
        idx2 = [sb(f"idx2{d}", [P, T2 + 3 * G], i16) for d in (0, 1)]
        lo2 = [sb(f"lo2{d}", [P, T2 + 2 * G]) for d in (0, 1)]
        maps = sb("maps", [P, T2], i32)
        tile2 = [maps[64 * d:64 * d + 1, :] for d in (0, 1)]
        rel2 = [maps[64 * d + 32:64 * d + 33, :] for d in (0, 1)]
        M = sb("M", [NL, NT, H])
        n0, n1 = (sb(f"n{k}", [NL, NT, H]) for k in range(2))
        stat = sb("stat", [NL, NT, 4])
        ADC = sb("ADC", [NL, NT, 2 * H])
        used = sb("used", [P, 2], i32)
        arena = sb("arena", [P, ARENA])
        taken_words = [0]

        def place(words, at=None):
            if at is not None:
                taken_words[0] = at
            taken_words[0] += words
            assert taken_words[0] <= ARENA, taken_words[0]
            return arena[:, taken_words[0] - words:taken_words[0]]

        idxc = sb("idxc", [P, 8], i32)
        row = place(8 * D, 0)[0:1, :].rearrange("p (k f) -> p k f", k=8)
        bc_att = place(2 * D, 0).rearrange("p (k f) -> p k f", k=2)
        prod = place(2 * D).rearrange("p (c f) -> p c f", c=2)
        stab = place(NT * 3 * H // 2)[0:NL, :].bitcast(bf16).rearrange("p (t k) -> p t k", t=NT)
        place_oh = place(6 * (P // 2)).bitcast(f16).rearrange("p (u s) -> p u s", u=6)
        assert taken_words[0] <= 8 * D
        place(0, 8 * D)
        xs = place(2 * D)[0:NL, :].rearrange("p (u f) -> p u f", u=2)
        xT = place(4 * NL).rearrange("p (u k) -> p u k", u=2)
        place(0, 8 * D + 2 * D)
        lab = place(8 * P).bitcast(f16).rearrange("p (u k s) -> p u k s", u=8, k=2)
        dmap, onesw, typ1 = place(T1), place(T1), place(T1)
        sel = place(H * P // 2, 4856).bitcast(bf16).rearrange("p (h n) -> p h n", h=H)
        nbig = place(G * P // 2).bitcast(bf16).rearrange("p (u n) -> p u n", u=G)
        sring = place(8 * 3 * H // 2, 0).bitcast(bf16).rearrange("p (u k) -> p u k", u=8)
        asT = place(2 * P // 2).bitcast(bf16).rearrange("p (u e) -> p u e", u=2)
        mx = place(8 * H)[0:NL, :].rearrange("p (u h) -> p u h", u=8)
        noh = place(4 * (NL // 2)).bitcast(bf16).rearrange("p (u n) -> p u n", u=4)
        idxs = place(4 * G, 0).bitcast(i32)
        oh = place(4 * G * NL).rearrange("p (u n) -> p u n", u=4 * G)
        ohT = place(G * P)[0:NL, :].rearrange("p (u e) -> p u e", u=G)
        small = place(3 * G * H).rearrange("p (k m) -> p k m", k=3)
        upper = WR[:, 2 * R * D:4 * R * D]
        scaled = upper[:, 0:2 * G * HW].rearrange("p (u f) -> p u f", u=2 * G)
        ring = upper[:, 2 * G * HW:6 * G * HW].rearrange("p (u f) -> p u f", u=4 * G)
        looped = WR[0:NL, 0:NT * D].rearrange("p (t f) -> p t f", t=NT)
        low = place(NT * D // 2, 0)[0:NL, :].bitcast(bf16).rearrange("p (t f) -> p t f", t=NT)
        xring = place(8 * 3 * D // 2, 0).bitcast(bf16).rearrange("p (u f) -> p u f", u=8)
        att = place(8 * 2 * NL).rearrange("p (u k) -> p u k", u=8)
        ohb = place(8 * (NL // 2)).bitcast(bf16).rearrange("p (u n) -> p u n", u=8)
        Wl = place(2 * D, 5400).rearrange("p (c o) -> p c o", c=2)
        PS = ctx.enter_context(nc.psum_tensor("PS", [P, 8, 512], f32))

        at = [0]

        def cut(words):
            at[0] += words
            assert at[0] <= 2 * R * 2 * D
            return WR[:, at[0] - words:at[0]]

        own_i, oth_i, typ_i = (cut(C0).bitcast(i32) for _ in range(3))
        hi, lo, t0, t1, t2, pos, jf, sf = (cut(T1) for _ in range(8))
        AB0 = cut(2 * T1).rearrange("p (c k) -> p c k", k=2)
        Av, Bv = AB0[:, :, 0], AB0[:, :, 1]
        rowtot, offs, r0, r1 = (cut(NT) for _ in range(4))
        c0, c1, c2, c3 = (cut(1) for _ in range(4))
        AB1 = cut(2 * T1).rearrange("p (c k) -> p c k", k=2)
        A1, B1 = AB1[:, :, 0], AB1[:, :, 1]

        masks = cut(R * T1 // 2).bitcast(f16).rearrange("p (t j) -> p t j", t=R)
        cntj = cut(4 * R)
        dT = cut(4 * NT)
        cnt, end2, s0, s1 = (cut(R) for _ in range(4))
        shift = cut(R + 2)
        shiftb = cut(4 * P).rearrange("p (u e) -> p u e", u=4)
        ohj = cut(8 * (T2 // 2)).bitcast(f16).rearrange("p (u j) -> p u j", u=8)
        q0, q1 = cut(T2), cut(T2)
        iota_i = q0.bitcast(i32)
        trif, triif = cut(P), cut(P)
        tri16, ones16, zero16 = (cut(P // 2).bitcast(f16) for _ in range(3))
        parts = ACC[1][:, :, 0:D].bitcast(bf16)

        gate = sem("gate")
        filled = sem("filled")
        made = sem("made")
        x_padded = sem("x_padded")
        wl_in = sem("wl_in")
        x_in, w_in, rows_in, wr_in = sem("x_in"), sem("w_in"), sem("rows_in"), [sem(f"wr_in{d}") for d in (0, 1)]
        edges_in = [sem(f"edges_in{d}") for d in (0, 1)]
        vs = sem("vs")
        spread = sem("spread")
        wg_ready = sem("wg_ready")
        lin1, lin2 = ([sem(f"{name}{k}") for name in ("x_copied", "x_turned", "xt_ready", "multiplied", "product_out")] for k in (1, 2))
        product_out1, product_out2 = lin1[4], lin2[4]
        sort_in, sort_out = sem("sort_in"), sem("sort_out")
        place_ready, own_weighed, perm_in, perm_out = sem("place_ready"), sem("own_weighed"), sem("perm_in"), sem("perm_out")
        sort_done = sem("sort_done")
        tab_ready = sem("tab_ready")
        h_out, s_out, x_out = sem("h_out"), sem("s_out"), sem("x_out")
        gath = [sem(f"gath{u}") for u in range(8)]
        idx_ready = sem("idx_ready")
        gath_h = [sem(f"gath_h{u}") for u in range(4 * G)]
        idxs_ready = sem("idxs_ready")
        noh_ready, turned, ast_ready = sem("noh_ready"), sem("turned"), sem("ast_ready")
        v_done, max_taken = sem("v_done"), sem("max_taken")
        oh_ready, oht_ps, oht_ready = sem("oh_ready"), sem("oht_ps"), sem("oht_ready")
        adc_done, z_ready, p_ready = sem("adc_done"), sem("z_ready"), sem("p_ready")
        hp_ready, agg_done, acc_taken = sem("hp_ready"), sem("agg_done"), sem("acc_taken")
        shift_ready, self_exp = sem("shift_ready"), sem("self_exp")
        gath2 = [[sem(f"gath2{d}{u}") for u in range(8)] for d in (0, 1)]
        idx2_ready = [sem(f"idx2_ready{d}") for d in (0, 1)]
        roh_ready = [sem(f"roh_ready{d}") for d in (0, 1)]
        at_ps = [sem(f"at_ps{d}") for d in (0, 1)]
        at_ready = [sem(f"at_ready{d}") for d in (0, 1)]
        y_done = [sem(f"y_done{d}") for d in (0, 1)]
        y_taken = [sem(f"y_taken{d}") for d in (0, 1)]
        over = [sem(f"over{d}") for d in (0, 1)]
        ln_act, ln_in = sem("ln_act"), sem("ln_in")
        out_ready, out_done = sem("out_ready"), sem("out_done")

        block = ctx.enter_context(nc.Block())

        def loads(eng, which, row_, top):
            _, values = nc.values_load_multi_w_load_instructions(
                row_, engines=[which], min_val=0, max_val=top,
                skip_runtime_bounds_check_because="VectorE has bounded them")
            return values

        def node_rows(t):
            return t.rearrange("(t p) f -> p t f", p=NL)

        WV = WR[:, :].rearrange("p (d r c o) -> p d r c o", d=2, r=R, c=2)

        def tiles_of(rows, t):
            whole = (NT - 1) * NL
            return ((node_rows(rows[0:whole, :]), t[:, 0:NT - 1, 0:D]),
                    (rows[whole:N, :], t[0:LAST, NT - 1:NT, 0:D].rearrange("p t f -> p (t f)")))

        @block.sync
        def _(sp):
            for k, name in enumerate(("L0_gnn_att_src", "L0_gnn_att_dst", "L0_gnn_bias", "L0_gnn_ln_gamma", "L0_gnn_ln_beta",
                                      "L1_gnn_forward_bias", "L1_gnn_backward_bias", "L1_gnn_self_bias")):
                v = a[name].rearrange("h c -> (h c)") if k < 2 else a[name]
                sp.dma_start(row[:, k, :], v.rearrange("(a n) -> a n", a=1)).then_inc(rows_in, 16)
            sp.wait_ge(x_padded, 1)
            sp.dma_start(Wg[:, :, 0:D], a["L0_gnn_W"].rearrange("(c p) o -> p c o", p=P)).then_inc(w_in, 16)
            for rows, x_rows in tiles_of(a["x"], X):
                sp.dma_start(x_rows, rows).then_inc(x_in, 16)
            for d, names in enumerate((("dst", "src"), ("src", "dst"))):
                sp.wait_ge(made, d + 1)
                for buf, name in zip((own_i, oth_i, typ_i), (*names, "edge_type_16")):
                    sp.dma_start(buf[0:FULL, :], a[name][0:FULL * C0].rearrange("(p c) -> p c", c=C0)).then_inc(edges_in[d], 16)
                    sp.dma_start(buf[FULL:FULL + 1, 0:REST],
                                 a[name][FULL * C0:E].rearrange("(p c) -> p c", p=1)).then_inc(edges_in[d], 16)
                if d == 0:
                    sp.wait_ge(product_out1, NT)
                    sp.dma_start(node_rows(h_table), Hn[:, :, 0:HW]).then_inc(h_out, 16)
                    sp.wait_ge(tab_ready, 1)
                    sp.dma_start(node_rows(s_table), stab).then_inc(s_out, 16)
            sp.wait_ge(sort_done, 2)
            def weights(d, name):
                for c in range(2):
                    sp.dma_start(WV[:, d, :, c, :], a[name][:, c * P:(c + 1) * P, :].rearrange("r p o -> p r o")).then_inc(wr_in[d], 16)

            weights(0, "L1_gnn_Wf")
            sp.wait_ge(tab_ready, 2)
            sp.dma_start(Wl, a["L1_gnn_loop_weight"].rearrange("(c p) o -> p c o", p=P)).then_inc(wl_in, 16)
            sp.dma_start(node_rows(x_table[:, 0:2 * D]), parts).then_inc(x_out, 16)
            sp.dma_start(node_rows(x_table[:, 2 * D:3 * D]), low).then_inc(x_out, 16)
            weights(1, "L1_gnn_Wb")
            sp.wait_ge(out_ready, 1)
            for rows, result in tiles_of(out, ACC[0]):
                sp.dma_start(rows, result).then_inc(out_done, 16)
            sp.wait_ge(out_done, 32)

        @block.gpsimd
        def _(pool):
            pool.iota(iota_i[:, :], [[1, T2]], base=0, channel_multiplier=0).then_inc(filled, 1)
            pool.iota(pidx_i[:, :], [[1, 1]], base=0, channel_multiplier=1).then_inc(filled, 1)
            pool.memset(identf[:, :], 0.0).then_inc(filled, 1)
            pool.memset(identb[:, :], 0.0).then_inc(filled, 1)
            pool.memset(trif[:, :], 1.0).then_inc(filled, 1)
            pool.memset(triif[:, :], 1.0).then_inc(filled, 1)
            pool.memset(sel[:, :, :], 0.0).then_inc(filled, 1)
            pool.memset(nbig[:, :, :], 0.0).then_inc(filled, 1)
            pool.wait_ge(filled, 8)
            for m in (identf, identb):
                pool.affine_select(out=m[:, :], in_=m[:, :], compare_op=ALU.not_equal, fill=1.0, base=0,
                                   pattern=[[-1, P]], channel_multiplier=1).then_inc(filled, 1)
            pool.affine_select(out=trif[:, :], in_=trif[:, :], compare_op=ALU.is_gt, fill=0.0, base=0,
                               pattern=[[1, P]], channel_multiplier=-1).then_inc(filled, 1)
            pool.affine_select(out=triif[:, :], in_=triif[:, :], compare_op=ALU.is_ge, fill=0.0, base=0,
                               pattern=[[1, P]], channel_multiplier=-1).then_inc(filled, 1)
            pool.affine_select(out=nbig[:, :, :], in_=nbig[:, :, :], compare_op=ALU.not_equal, fill=ABSENT, base=0,
                               pattern=[[0, G], [-1, P]], channel_multiplier=1).then_inc(filled, 1)
            for m in range(3):
                pool.affine_select(out=sel[:, :, :], in_=sel[:, :, :], compare_op=ALU.not_equal, fill=1.0, base=-H * m,
                                   pattern=[[-1, H], [0, P]], channel_multiplier=1).then_inc(filled, 1)
                pool.wait_ge(filled, 14 + m)

            pool.wait_ge(s_out, 16)
            with pool.Fori(0, T1 // 8) as i:
                for u in range(8):
                    if u % G == 0:
                        pool.wait_ge(idx_ready, 2 * i + u // G + 1)
                    pool.wait_ge(turned, 8 * i + u + 1)
                    pool.sem_inc(gate, 1)
                    pool.indirect_dma_start(out=sring[:, u, :], out_offset=None, in_=s_table,
                                            in_offset=bass.IndirectOffsetOnAxis(ap=idxc[:, u:u + 1], axis=0)
                                            ).then_inc(gath[u], 16)
            pool.wait_ge(h_out, 16)

            def h_rows(i, q):
                pool.wait_ge(idxs_ready, 4 * i + q + 1)
                for u in range(G * q, G * q + G):
                    pool.wait_ge(hp_ready, 4 * G * i + u + 1)
                    pool.sem_inc(gate, 1)
                    pool.indirect_dma_start(out=ring[:, u, :], out_offset=None, in_=h_table,
                                            in_offset=bass.IndirectOffsetOnAxis(ap=idxs[:, u:u + 1], axis=0)
                                            ).then_inc(gath_h[u], 16)

            with pool.Fori(0, ROUNDS) as i:
                for q in range(4):
                    h_rows(i, q)
            for q in range(TAIL):
                h_rows(ROUNDS, q)
            pool.wait_ge(x_out, 32)
            for d in (0, 1):
                if d:
                    pool.wait_ge(over[0], 3)

                def x_rows(i, g):
                    pool.wait_ge(idx2_ready[d], 2 * i + g + 1)
                    for u in range(G * g, G * g + G):
                        pool.wait_ge(at_ps[d], 8 * i + u + 1)
                        pool.sem_inc(gate, 1)
                        pool.indirect_dma_start(out=xring[:, u, :], out_offset=None, in_=x_table,
                                                in_offset=bass.IndirectOffsetOnAxis(ap=idxc[:, u:u + 1], axis=0)
                                                ).then_inc(gath2[d][u], 16)

                limit = pool.value_load(used[0:1, d:d + 1], min_val=1, max_val=T2)
                x_rows(0, 0)
                with pool.Fori(0, T2 // 8 // BLOCK) as block_:
                    with pool.If(block_ * (8 * BLOCK) < limit):
                        with pool.Fori(0, BLOCK) as j_:
                            i = block_ * BLOCK + j_
                            with pool.If(i * 8 < limit):
                                x_rows(i, 1)
                                x_rows(i + 1, 0)

        @block.scalar
        def _(act):
            def around_products(sems, put):
                x_copied, x_turned, xt_ready, multiplied, _ = sems

                def copy_x(t, u):
                    act.wait_ge(x_turned, t)
                    act.sem_inc(gate, 1)
                    act.activation(xs[:, u % 2, :], X[:, ds(t, 1), :].rearrange("p a f -> p (a f)"), ACT.Copy).then_inc(x_copied, 1)

                def tile(t, u, last=False):
                    if not last:
                        copy_x(t + 1, u + 1)
                    act.wait_ge(x_turned, t + 2)
                    act.activation(xT[:, u, :], PS[:, TURN_BANKS[u], 0:2 * NL], ACT.Copy).then_inc(xt_ready, 1)
                    act.wait_ge(multiplied, t + 1)
                    act.sem_inc(gate, 1)
                    put(t)

                act.activation(xs[:, 0, :], X[:, 0, :], ACT.Copy).then_inc(x_copied, 1)
                with act.Fori(0, NT // 2 - 1) as i:
                    for u in range(2):
                        tile(2 * i + u, u)
                for u in range(2):
                    tile(NT - 2 + u, u, last=u == 1)

            act.wait_ge(x_in, 32)
            act.wait_ge(spread, 1)
            around_products(lin1, lambda t: act.activation(Hn[:, ds(t, 1), :].rearrange("p a f -> p (a f)"), PS[0:NL, 1, 0:XW], ACT.Copy)
                            .then_inc(product_out1, 1))

            def indices(idx, ready, group, half):
                act.activation(idxc[:, half * G:(half + 1) * G], idx[:, ds(group * G, G)], ACT.Copy).then_inc(ready, 1)

            def gathers_done(sems, times, half):
                for u in range(half * G, (half + 1) * G):
                    act.wait_ge(sems[u], 16 * times)
                act.sem_inc(gate, 1)

            weighed = 0
            for k, (cols, ab) in enumerate(((C0, AB0), (T1, AB1)) * 2):
                with act.Fori(0, cols // 8) as i:
                    for u in (0, 1, 2, 4, 5, 6):
                        act.wait_ge(place_ready, weighed + 6 * i + u - u // 4 + 1)
                        act.sem_inc(gate, 1)
                        act.activation(lab[:, u, 0, :], place_oh[:, u - u // 4, :], ACT.Copy, scale=ab[:, ds(8 * i + u, 1), 0])
                        act.activation(lab[:, u, 1, :], place_oh[:, u - u // 4, :], ACT.Copy, scale=ab[:, ds(8 * i + u, 1), 1]).then_inc(perm_in, 1)
                weighed += 3 * (cols // 4)
            act.wait_ge(sort_done, 3)
            indices(idx1, idx_ready, 0, 0)
            indices(idx1, idx_ready, 1, 1)

            def distances(n, u):
                act.activation(noh[:, u % 4, :], iota16[:, 1:NL + 1], ACT.Abs, scale=-1.0, bias=lo1[:, ds(n, 1)]).then_inc(noh_ready, 1)

            for u in range(2):
                distances(u, u)
            with act.Fori(0, T1 // 8) as i:
                for u in range(8):
                    act.wait_ge(turned, 8 * i + u + 9)
                    act.wait_ge(v_done, 8 * i + u + 1)
                    act.activation(asT[0:3 * H, u % 2, :], PS[0:3 * H, 4 + u % 2, 0:P // 2].bitcast(bf16), ACT.Copy).then_inc(ast_ready, 1)
                    distances(8 * i + u + 2, u + 2)
                    if u % G == G - 1:
                        gathers_done(gath, i + 1, u // G)
                        indices(idx1, idx_ready, 2 * i + 2 + u // G, u // G)
            act.wait_ge(shift_ready, 1)
            act.activation(n1[:, :, :], n0[:, :, :], ACT.Exp).then_inc(self_exp, 1)
            def h_indices(g, q):
                act.activation(idxs[:, G * q:G * q + G], idx1[:, ds(g * G, G)], ACT.Copy).then_inc(idxs_ready, 1)

            for q in range(4):
                h_indices(q, q)

            def turned_onehots(g, q):
                act.wait_ge(oht_ps, g + 1)
                act.wait_ge(adc_done, G * g + G)
                act.activation(ohT, PS[0:NL, q % 2, :].rearrange("p (u e) -> p u e", u=G), ACT.Copy).then_inc(oht_ready, 1)

            def exps(i, q, ahead):
                g = 4 * i + q
                act.wait_ge(z_ready, g + 1)
                act.wait_ge(agg_done, G * g + G)
                act.activation(scaled[:, G * (q % 2):G * (q % 2) + G, D:HW], small[:, 2, :].rearrange("p (u h) -> p u h", u=G), ACT.Exp).then_inc(p_ready, 1)
                if ahead:
                    turned_onehots(g + 2, q + 2)
                if i is not ROUNDS:
                    gathers_done(gath_h, i + 1, q)
                    h_indices(g + 4, q)

            for q in range(2):
                turned_onehots(q, q)
            with act.Fori(0, ROUNDS - 1) as i:
                for q in range(4):
                    exps(i, q, True)
            for q in range(4 + TAIL):
                exps(ROUNDS if q > 3 else ROUNDS - 1, q % 4, q < 2 + TAIL)
            for k in range(2):
                act.wait_ge(ln_in, k + 1)
                act.activation(stat[:, :, 3], stat[:, :, 2], ACT.Sqrt).then_inc(ln_act, 1)
            for d in (0, 1):
                if d == 0:
                    act.wait_ge(idx_ready, T1 // G + 2)
                else:
                    act.wait_ge(over[0], 3)
                indices(idx2[d], idx2_ready[d], 0, 0)
                indices(idx2[d], idx2_ready[d], 1, 1)

                def turned_sums(i, g):
                    gathers_done(gath2[d], i + 1, g)
                    indices(idx2[d], idx2_ready[d], 2 * i + 2 + g, g)
                    for b in range(2):
                        n = 8 * i + G * g + 2 * b
                        act.wait_ge(at_ps[d], n + 2 + 8)
                        act.wait_ge(y_done[d], n + 2)
                        act.activation(att[:, G * g + 2 * b:G * g + 2 * b + 2, :],
                                       PS[:, 2 * g + b, :].rearrange("p (u k) -> p u k", u=2)[:, :, 0:2 * NL],
                                       ACT.Copy).then_inc(at_ready[d], 2)

                limit = act.value_load(used[0:1, d:d + 1], min_val=1, max_val=T2)
                turned_sums(0, 0)
                with act.Fori(0, T2 // 8 // BLOCK) as block_:
                    with act.If(block_ * (8 * BLOCK) < limit):
                        with act.Fori(0, BLOCK) as j_:
                            i = block_ * BLOCK + j_
                            with act.If(i * 8 < limit):
                                turned_sums(i, 1)
                                turned_sums(i + 1, 0)
                act.drain().then_inc(over[d], 1)
            act.wait_ge(over[1], 3)
            around_products(lin2, lambda t: act.activation(looped[:, ds(t, 1), :].rearrange("p a f -> p (a f)"), PS[0:NL, 1, 0:D], ACT.Copy,
                                                           scale=2.0).then_inc(product_out2, 1))
            act.wait_ge(ln_in, 3)
            act.activation(stat[:, :, 3], stat[:, :, 2], ACT.Sqrt).then_inc(ln_act, 1)

        @block.tensor
        def _(pe):
            def mm(*args, **kw):
                return pe.matmul(*args, **kw)

            def products_of(sems, weights, width):
                x_copied, x_turned, xt_ready, multiplied, _ = sems

                def turn_x(t, u):
                    pe.wait_ge(x_copied, t + 1)
                    for c in range(2):
                        last = pe.transpose(PS[:, TURN_BANKS[u % 2], c * NL:(c + 1) * NL], xs[:, u % 2, c * P:(c + 1) * P], identf[0:NL, 0:NL])
                    last.then_inc(x_turned, 1)

                def tile(t, u, last=False):
                    if not last:
                        turn_x(t + 1, u + 1)
                    pe.wait_ge(xt_ready, t + 1)
                    for c in range(2):
                        last_ = mm(PS[0:NL, 1, 0:width], xT[:, u, c * NL:(c + 1) * NL], weights[:, c, :], start=c == 0, stop=c == 1)
                    last_.then_inc(multiplied, 1)

                pe.sem_inc(x_turned, 1)
                turn_x(0, 0)
                with pe.Fori(0, NT // 2 - 1) as i:
                    for u in range(2):
                        tile(2 * i + u, u)
                for u in range(2):
                    tile(NT - 2 + u, u, last=u == 1)

            pe.wait_ge(made, 1)
            pe.wait_ge(rows_in, 128)
            for k in range(4):
                for m in range(2):
                    last = mm(PS[:, 2 + k, m * D:(m + 1) * D], onesf[0:1, :], row[0:1, 2 * k + m, :], start=True, stop=True)
            last.then_inc(spread, 1)
            si, so = Steps(sort_in), Steps(sort_out)
            pi, ow = Steps(perm_in), Steps(own_weighed)

            def permute(cols, width, limit=None):
                pieces = [(h, min(width, h + NARROW)) for h in range(0, width, NARROW)]

                def plane(k, piece, weights, rows, **kw):
                    lo_, hi_ = piece
                    return mm(PS[:, 4 + k * 2 + lo_ // NARROW, 0:hi_ - lo_], weights, rows[:, lo_:hi_], **kw)

                def columns(pieces):
                    with pe.Fori(0, cols // 8) as i:
                        for u in range(8):
                            if u % 4 < 3:
                                pe.wait_ge(perm_in, pi.base + 6 * i + u - u // 4 + 1)
                            else:
                                pe.wait_ge(own_weighed, ow.base + 2 * i + u // 4 + 1)
                            for k in range(2):
                                for piece in pieces:
                                    last = plane(k, piece, lab[:, u, k, :], ohj[:, u, :], start=False, stop=False)
                            last.then_inc(perm_out, 1)

                for k in range(2):
                    for piece in pieces:
                        last = plane(k, piece, zero16[:, :], iota16, start=True, stop=False)
                last.then_inc(perm_out, 8)
                if limit is None:
                    columns(pieces)
                else:
                    with pe.If(limit < NARROW + 1):
                        columns(pieces[:1])
                    with pe.If(limit > NARROW):
                        columns(pieces)
                pi.base += 3 * (cols // 4)
                ow.base += cols // 4
                for k in range(2):
                    for piece in pieces:
                        last = plane(k, piece, zero16[:, :], iota16, start=False, stop=True)
                last.then_inc(perm_out, 1)

            for d in (0, 1):
                pe.wait_ge(sort_in, si.step())
                mm(PS[:, 2, 0:NT], onesf[:, :], rowtot, start=True, stop=True)
                mm(PS[:, 2, 32:32 + NT], trif[:, :], rowtot, start=True, stop=True)
                mm(PS[0:NT, 2, 64:65], rowtot, onesf[:, 0:1], start=True, stop=True).then_inc(sort_out, 1)
                pe.wait_ge(sort_in, si.step())
                mm(PS[0:NT, 2, 65:66], triif[0:NT, 0:NT], c1[0:NT, :], start=True, stop=True).then_inc(sort_out, 1)
                pe.wait_ge(sort_in, si.step())
                mm(PS[:, 3, 0:T1], ones16[0:NT, :], ohj[0:NT, 0, 0:T1], start=True, stop=True).then_inc(sort_out, 1)
                if d == 0:
                    pe.wait_ge(wg_ready, 1)
                    products_of(lin1, Wg, XW)
                    pe.wait_ge(product_out1, NT)
                pe.wait_ge(sort_in, si.step())
                permute(C0, T1)
                pe.wait_ge(sort_in, si.step())
                with pe.Fori(0, R) as t:
                    for k in range(4):
                        last = mm(PS[0:T1 // 4, 2, ds(t + 16 * k, 1)], masks[:, ds(t, 1), k * (T1 // 4):(k + 1) * (T1 // 4)].rearrange("p a j -> p (a j)"),
                                  ones16[:, 0:1], start=True, stop=True)
                last = mm(PS[0:1, 2, 64:65], ones16[:, 0:1], ones16[:, 0:1], start=True, stop=True)
                last.then_inc(sort_out, 1)
                pe.wait_ge(sort_in, si.step())
                for k in range(4):
                    last = mm(PS[0:NT, 2, 128:128 + R], dT[0:T1 // 4, k * NT:(k + 1) * NT], cntj[0:T1 // 4, k * R:(k + 1) * R], start=k == 0, stop=k == 3)
                last.then_inc(sort_out, 1)
                pe.wait_ge(sort_in, si.step())
                mm(PS[0:NT, 2, 160:160 + R], trif[0:NT, 0:NT], cnt[0:NT, :], start=True, stop=True)
                mm(PS[0:NT, 2, 176:177], trif[0:NT, 0:NT], end2[0:NT, R - 1:R], start=True, stop=True).then_inc(sort_out, 1)
                for t in range(R):
                    if t % 8 == 0:
                        pe.wait_ge(sort_in, si.step())
                    for h in range(2):
                        behind = ohj[0:NT, t % 8, h * (T2 // 2):(h + 1) * (T2 // 2)]
                        last = mm(PS[:, h, 0:T2 // 2], ones16[0:NT, :], behind, start=t == 0, stop=t == R - 1)
                        if t == R - 1:
                            last = mm(PS[:, 4 + h, 0:T2 // 2], ones16[0:NT, :], behind, start=True, stop=True)
                    if t % 8 == 7:
                        last.then_inc(sort_out, 1)
                a0 = si.base
                with pe.Fori(0, R // 4) as i:
                    for k in range(4):
                        t = 4 * i + k
                        pe.wait_ge(sort_in, a0 + t + 1)
                        mask = masks[:, ds(t, 1), :].rearrange("p a j -> p (a j)")
                        mm(PS[:, PLACE_BANKS[k], 0:T1], tri16[:, :], mask, start=True, stop=False)
                        mm(PS[:, PLACE_BANKS[k], 0:T1], shiftb[0:NT, k, :], dmap[0:NT, :], start=False, stop=True)
                        mm(PS[:, COLUMN_BANKS[k], 0:T1], ones16[:, :], mask, start=True, stop=True).then_inc(sort_out, 1)
                si.base += R + 2
                pe.wait_ge(sort_in, si.step())
                permute(T1, T2, pe.value_load(used[0:1, d:d + 1], min_val=1, max_val=T2))

            pe.wait_ge(sort_done, 3)
            pe.sem_inc(v_done, 2)
            pe.sem_inc(turned, 8)

            def turn(i, u):
                pe.wait_ge(gath[u], 16 * (i + 1))
                if not (isinstance(i, int) and 8 * i + u < 2):
                    pe.wait_ge(ast_ready, 8 * i + u - 1)
                pe.transpose(PS[0:3 * H, 4 + u % 2, 0:P // 2].bitcast(bf16), sring[:, u, :], identb[:, :]).then_inc(turned, 1)

            def values(i, u):
                pe.wait_ge(noh_ready, 8 * i + u + 1)
                pe.wait_ge(max_taken, 8 * i + u + 1)
                for b in range(2):
                    mm(PS[0:NL, (u % 2) * 2 + b, :], noh[:, u % 4, :], nbig[:, :, :].rearrange("p a b -> p (a b)"), start=True, stop=False)
                pe.wait_ge(ast_ready, 8 * i + u + 1)
                for h in range(H):
                    last = mm(PS[0:NL, (u % 2) * 2 + h // 4, (h % 4) * P:(h % 4 + 1) * P], sel[:, h, 0:NL], asT[:, u % 2, :],
                              start=False, stop=h % 4 == 3)
                last.then_inc(v_done, 1)

            turn(0, 0)
            for u in range(8):
                if u < 7:
                    turn(0, u + 1)
                else:
                    turn(1, 0)
                values(0, u)
            with pe.Fori(1, T1 // 8 - 1) as i:
                for u in range(8):
                    if u < 7:
                        turn(i, u + 1)
                    else:
                        turn(i + 1, 0)
                    values(i, u)
            for u in range(8):
                if u < 7:
                    turn(T1 // 8 - 1, u + 1)
                values(T1 // 8 - 1, u)

            pe.wait_ge(shift_ready, 1)
            pe.sem_inc(adc_done, G)
            pe.sem_inc(agg_done, 2 * G)

            def turn_onehots(g, q):
                pe.wait_ge(oh_ready, G * g + G)
                for u in range(G):
                    last = pe.transpose(PS[0:NL, q % 2, u * P:(u + 1) * P], oh[:, (G * q + u) % (4 * G), :], identf[:, :])
                last.then_inc(oht_ps, 1)

            def to_edges(g, q):
                tiles = loads(pe, mybir.EngineType.PE, tile1[0:1, ds(G * g, G)], NT - 1)
                pe.wait_ge(oht_ready, g + 1)
                for u in range(G):
                    mm(PS[:, 2 + q % 2, u * 2 * H:(u + 1) * 2 * H], ohT[:, u, :], ADC[:, ds(tiles[u], 1), :].rearrange("p a k -> p (a k)"),
                       start=True, stop=True).then_inc(adc_done, 1)

            def sums(i, q, ahead):
                g = 4 * i + q
                if ahead:
                    turn_onehots(g + 2, q + 2)
                for u in range(G):
                    pe.wait_ge(hp_ready, 4 * G + G * g + u + 1)
                    pe.wait_ge(acc_taken, G * g + u + 1)
                    mm(PS[0:NL, 4 + u, 0:HW], oh[:, G * q + u, :], scaled[:, G * (q % 2) + u, :], start=True, stop=True).then_inc(agg_done, 1)
                if ahead:
                    to_edges(g + 2, q + 2)

            for q in range(2):
                turn_onehots(q, q)
            for q in range(2):
                to_edges(q, q)
            with pe.Fori(0, ROUNDS - 1) as i:
                for q in range(4):
                    sums(i, q, True)
            for q in range(4 + TAIL):
                sums(ROUNDS - 1 + q // 4, q % 4, q < 2 + TAIL)

            for d in (0, 1):
                pe.wait_ge(wr_in[d], 32)
                if d:
                    pe.wait_ge(over[0], 3)
                else:
                    pe.wait_ge(x_out, 32)
                pe.sem_inc(y_done[d], 8)
                pe.sem_inc(at_ps[d], 8)

                def row_sums(i, g):
                    for u in range(G):
                        n = 8 * i + G * g + u
                        b = g * 2 + u // 2
                        pe.wait_ge(gath2[d][G * g + u], 16 * (i + 1))
                        pe.wait_ge(roh_ready[d], n + 1)
                        for c in range(2):
                            for k in range(3):
                                last = mm(PS[:, b, (u % 2) * 256 + c * NL:(u % 2) * 256 + (c + 1) * NL],
                                          xring[:, G * g + u, k * D + c * P:k * D + (c + 1) * P], ohb[:, G * g + u, :], start=k == 0, stop=k == 2)
                        last.then_inc(at_ps[d], 1)

                def relations_of(i, g):
                    return loads(pe, mybir.EngineType.PE, rel2[d][0:1, ds(8 * i + G * g, G)], R - 1)

                def products(i, g, rels):
                    for u in range(G):
                        n = 8 * i + G * g + u
                        pe.wait_ge(at_ready[d], n + 1)
                        pe.wait_ge(y_taken[d], n + 1)
                        for c in range(2):
                            mm(PS[0:NL, 4 + u, 0:D], att[:, G * g + u, c * NL:(c + 1) * NL],
                               WV[:, d, ds(rels[u], 1), c, :].rearrange("p a o -> p (a o)"), start=c == 0, stop=c == 1)
                        mm(PS[0:NL, 4 + u, D:D + 1], ohb[:, G * g + u, :], onesb[:, 0:1], start=True, stop=True).then_inc(y_done[d], 1)

                limit = pe.value_load(used[0:1, d:d + 1], min_val=1, max_val=T2)
                row_sums(0, 0)
                with pe.Fori(0, T2 // 8 // BLOCK) as block_:
                    with pe.If(block_ * (8 * BLOCK) < limit):
                        with pe.Fori(0, BLOCK) as j_:
                            i = block_ * BLOCK + j_
                            with pe.If(i * 8 < limit):
                                rels = relations_of(i, 0)
                                row_sums(i, 1)
                                products(i, 0, rels)
                                rels = relations_of(i, 1)
                                row_sums(i + 1, 0)
                                products(i, 1, rels)
                pe.drain().then_inc(over[d], 1)
            pe.wait_ge(wl_in, 16)
            products_of(lin2, Wl, D)

        @block.vector
        def _(dve):
            S = Steps(vs)

            def v(ins):
                ins.then_inc(vs, 1)
                dve.wait_ge(vs, S.step())

            def lagged(ins):
                ins.then_inc(vs, 1)
                dve.wait_ge(vs, S.step() - 1)

            def every_tile(step):
                with dve.Fori(0, NT // 4) as i:
                    S.loop(i, 4)
                    for u in range(4):
                        step(4 * i + u).then_inc(vs, 1)
                        S.step()
                S.end(NT // 4)
                dve.wait_ge(vs, S.now)

            def ts(out, in_, s1, op0, s2=None, op1=ALU.bypass, **kw):
                return dve.tensor_scalar(out, in_, s1, s2, op0, op1, **kw)

            def stt(out, in0, s, in1, op0, op1):
                return dve.scalar_tensor_tensor(out=out, in0=in0, scalar=s, in1=in1, op0=op0, op1=op1)

            cp, tt = dve.tensor_copy, dve.tensor_tensor

            v(dve.memset(X[:, NT - 1, :], 0.0))
            dve.sem_inc(x_padded, 1)
            v(dve.memset(ones16[:, :], 1.0))
            v(dve.memset(onesf[:, :], 1.0))
            v(dve.memset(onesw[:, :], 1.0))
            v(dve.memset(onesb[:, :], 1.0))
            v(dve.memset(zero16[:, :], 0.0))
            for idx, w, pad in ((idx1, T1, 2 * G), (idx2[0], T2, 3 * G), (idx2[1], T2, 3 * G)):
                v(dve.memset(idx[:, w:w + pad], 0))
            for lo_, w in ((lo1, T1), (lo2[0], T2), (lo2[1], T2)):
                v(dve.memset(lo_[:, w:w + 2 * G], 0.0))
            v(dve.memset(own_i, 4000))
            v(dve.memset(oth_i, 0))
            v(dve.memset(typ_i, 0))
            dve.wait_ge(filled, 16)
            v(cp(iota16[:, :], iota_i[:, :]))
            v(cp(iotaf[:, :], iota_i[:, 0:P]))
            v(cp(pidx[:, :], pidx_i[:, :]))
            v(cp(tri16[:, :], trif[:, :]))
            dve.sem_inc(made, 1)
            dve.wait_ge(spread, 1)
            v(cp(bc_att, PS[:, 2, :].rearrange("p (k f) -> p k f", k=2)))
            v(cp(bc[:, :, :], PS[:, 3:6, :].rearrange("p b (k f) -> p (b k) f", k=2)))
            dve.wait_ge(w_in, 16)
            for k in range(2):
                v(tt(prod, Wg[:, :, 0:D],
                     bc_att[:, k:k + 1, :].broadcast_to([P, 2, D]), ALU.mult))
                v(dve.reduce_sum(Wg[:, :, D + k * H:D + (k + 1) * H],
                                 prod.rearrange("p c (h f) -> p c h f", h=H), AX.X))
            dve.sem_inc(wg_ready, 1)

            so = Steps(sort_out)
            perm = [0, 0]

            def ask():
                dve.sem_inc(sort_in, 1)
                dve.wait_ge(sort_out, so.step())

            def split(width, p):
                v(cp(t0[:, 0:width].bitcast(i32), p))
                v(ts(t1[:, 0:width].bitcast(i32), t0[:, 0:width].bitcast(i32), 7, ALU.logical_shift_right))
                v(ts(t2[:, 0:width].bitcast(i32), t0[:, 0:width].bitcast(i32), P - 1, ALU.bitwise_and))
                v(cp(jf[:, 0:width], t1[:, 0:width].bitcast(i32)))
                v(cp(sf[:, 0:width], t2[:, 0:width].bitcast(i32)))

            def permute(cols, width, ab, limit=None):
                def columns(width):
                    with dve.Fori(0, cols // 8) as i:
                        for u in range(8):
                            c = i * 8 + u
                            dve.wait_ge(perm_out, perm[1] + 8 * i + u + 1)
                            ts(ohj[:, u, 0:width], iota16[:, 0:width], jf[:, ds(c, 1)], ALU.is_equal)
                            if u % 4 < 3:
                                ts(place_oh[:, u - u // 4, :], iota16[:, 0:P], sf[:, ds(c, 1)], ALU.is_equal).then_inc(place_ready, 1)
                            else:
                                stt(lab[:, u, :, :], iota16[:, 0:P].rearrange("p (a s) -> p a s", a=1).broadcast_to([P, 2, P]), sf[:, ds(c, 1)],
                                    ab[:, ds(c, 1), :].rearrange("p a (k o) -> p (a k) o", o=1).broadcast_to([P, 2, P]),
                                    ALU.is_equal, ALU.mult).then_inc(own_weighed, 1)

                dve.sem_inc(sort_in, 1)
                if limit is None:
                    columns(width)
                else:
                    with dve.If(limit < NARROW + 1):
                        columns(NARROW)
                    with dve.If(limit > NARROW):
                        columns(width)
                perm[1] += 8 + cols + 1
                dve.wait_ge(perm_out, perm[1])

            def slots_of(dst, src):
                v(cp(dst.bitcast(i32), src))
                v(ts(dst.bitcast(i32), dst.bitcast(i32), P - 1, ALU.add))
                v(ts(dst.bitcast(i32), dst.bitcast(i32), 7, ALU.logical_shift_right))

            for d in (0, 1):
                cols = slice(0, C0)
                dve.wait_ge(edges_in[d], 96)
                v(cp(hi[:, cols], own_i))
                v(cp(Av[:, cols], oth_i))
                v(cp(Bv[:, cols], typ_i))
                v(ts(t0[:, cols], hi[:, cols], 1.0 / NL, ALU.mult, 0.5 / NL - 0.5, ALU.add))
                v(cp(jf[:, cols].bitcast(i32), t0[:, cols]))
                v(cp(t0[:, cols], jf[:, cols].bitcast(i32)))
                v(stt(t1[:, cols], t0[:, cols], -float(NL), hi[:, cols], ALU.mult, ALU.add))
                v(ts(t2[:, cols], t1[:, cols], float(NL), ALU.is_ge))
                v(ts(pos[:, cols], t1[:, cols], 0.0, ALU.is_lt))
                v(tt(t2[:, cols], t2[:, cols], pos[:, cols], ALU.subtract))
                v(tt(hi[:, cols], t0[:, cols], t2[:, cols], ALU.add))
                v(stt(lo[:, cols], t2[:, cols], -float(NL), t1[:, cols], ALU.mult, ALU.add))
                v(ts(lo[:, cols], lo[:, cols], 1.0, ALU.add, 16.0, ALU.mult))
                v(tt(Bv[:, cols], Bv[:, cols], lo[:, cols], ALU.add))
                v(ts(Av[:, cols], Av[:, cols], -float(OFF), ALU.add))
                if d == 0:
                    dve.wait_ge(edges_in[0], 96)
                with dve.Fori(0, NT // 2) as i:
                    S.loop(i, 2)
                    for k, junk in enumerate((t0, t1)):
                        lagged(ts(junk[:, cols], hi[:, cols], iotaf[:, ds(2 * i + k, 1)], ALU.is_equal, None, ALU.add,
                                  accum_out=rowtot[:, ds(2 * i + k, 1)]))
                S.end(NT // 2)
                dve.wait_ge(vs, S.now)
                ask()
                slots_of(r1, PS[:, 2, 0:NT])
                v(cp(offs, r1.bitcast(i32)))
                v(ts(r1, offs, 1.0, ALU.mult))
                v(dve.tensor_tensor_scan(r0, onesf[:, 0:NT], r1, 0.0, ALU.mult, ALU.add))
                v(tt(offs, r0, r1, ALU.subtract))
                v(stt(offs, offs, float(P), PS[:, 2, 32:32 + NT], ALU.mult, ALU.add))
                v(ts(offs, offs, -1.0, ALU.add))
                slots_of(c0[0:NT, :], PS[0:NT, 2, 64:65])
                v(cp(c1[0:NT, :], c0[0:NT, :].bitcast(i32)))
                ask()
                v(cp(c2[0:NT, :], PS[0:NT, 2, 65:66]))
                v(ts(ohj[0:NT, 0, 0:T1], iota16[0:NT, 0:T1], c2[0:NT, :], ALU.is_ge))
                ask()
                v(ts(q0[:, 0:T1], PS[:, 3, 0:T1], float(NT - 1), ALU.min))
                if d == 0:
                    v(cp(tile1[:, :], q0[:, 0:T1]))
                v(ts(dmap[0:NT, :], q0[0:NT, 0:T1], pidx[0:NT, :], ALU.is_equal))
                v(ts(pos[:, cols], hi[:, cols], float(NT), ALU.is_ge, FAR, ALU.mult))
                v(dve.memset(sf[:, cols], 0.0))
                with dve.Fori(0, NT // 2) as i:
                    S.loop(i, 8)
                    chains = ((t0, t1, pos), (t2, jf, sf))
                    for k, (there, count, to) in enumerate(chains):
                        lagged(ts(there[:, cols], hi[:, cols], iotaf[:, ds(2 * i + k, 1)], ALU.is_equal))
                    for k, (there, count, to) in enumerate(chains):
                        lagged(dve.tensor_tensor_scan(count[:, cols], onesw[:, cols], there[:, cols], offs[:, ds(2 * i + k, 1)], ALU.mult, ALU.add))
                    for k, (there, count, to) in enumerate(chains):
                        lagged(tt(count[:, cols], count[:, cols], there[:, cols], ALU.mult))
                    for k, (there, count, to) in enumerate(chains):
                        lagged(tt(to[:, cols], to[:, cols], count[:, cols], ALU.add))
                S.end(NT // 2)
                dve.wait_ge(vs, S.now)
                v(tt(pos[:, cols], pos[:, cols], sf[:, cols], ALU.add))
                split(C0, pos[:, cols])
                permute(C0, T1, AB0)
                v(cp(A1, PS[:, 4, 0:T1]))
                v(cp(B1, PS[:, 6, 0:T1]))
                v(cp(t0.bitcast(i32), B1))
                v(ts(t1.bitcast(i32), t0.bitcast(i32), 4, ALU.logical_shift_right))
                v(ts(t2.bitcast(i32), t0.bitcast(i32), R - 1, ALU.bitwise_and))
                v(cp(lo, t1.bitcast(i32)))
                v(cp(typ1, t2.bitcast(i32)))
                if d == 0:
                    v(ts(t0, lo, 0.0, ALU.is_equal, float(NONE - OFF), ALU.mult))
                    v(stt(idx1[:, 0:T1], A1, float(OFF), t0, ALU.add, ALU.add))
                    v(cp(lo1[:, 0:T1], lo))
                v(ts(t0, lo, 0.0, ALU.is_equal, 99.0, ALU.mult))
                v(tt(typ1, typ1, t0, ALU.add))
                with dve.Fori(0, R) as t:
                    S.loop(t, 1)
                    lagged(ts(masks[:, ds(t, 1), :].rearrange("p a j -> p (a j)"), typ1, iotaf[:, ds(t, 1)], ALU.is_equal))
                S.end(R)
                dve.wait_ge(vs, S.now)
                ask()
                q4 = T1 // 4
                v(cp(cntj[0:q4, :], PS[0:q4, 2, 0:4 * R]))
                for k in range(4):
                    v(ts(c3[0:q4, :], pidx[0:q4, :], float(q4 * k), ALU.add))
                    v(ts(q1[0:q4, 0:NT], r0[0:q4, :], c3[0:q4, :], ALU.is_le, None, ALU.add, accum_out=c0[0:q4, :]))
                    v(ts(c0[0:q4, :], c0[0:q4, :], float(NT - 1), ALU.min))
                    v(ts(dT[0:q4, k * NT:(k + 1) * NT], iotaf[0:q4, 0:NT], c0[0:q4, :], ALU.is_equal))
                ask()
                v(cp(cnt[0:NT, :], PS[0:NT, 2, 128:128 + R]))
                slots_of(s0[0:NT, :], cnt[0:NT, :])
                v(cp(s1[0:NT, :], s0[0:NT, :].bitcast(i32)))
                v(dve.tensor_tensor_scan(end2[0:NT, :], onesf[0:NT, 0:R], s1[0:NT, :], 0.0, ALU.mult, ALU.add))
                ask()
                v(cp(c2[0:NT, :], PS[0:NT, 2, 176:177]))
                v(ts(end2[0:NT, :], end2[0:NT, :], c2[0:NT, :], ALU.add))
                v(tt(shift[0:NT, 0:R], end2[0:NT, :], s1[0:NT, :], ALU.subtract))
                v(stt(shift[0:NT, 0:R], shift[0:NT, 0:R], float(P), PS[0:NT, 2, 160:160 + R], ALU.mult, ALU.subtract))
                for t in range(R):
                    lagged(ts(ohj[0:NT, t % 8, :], iota16[0:NT, :], end2[0:NT, t:t + 1], ALU.is_ge))
                    if t % 8 == 7:
                        dve.wait_ge(vs, S.now)
                        ask()
                halves = lambda x: x.rearrange("p (h j) -> p h j", h=2)
                v(ts(halves(q0), PS[:, 4:6, 0:T2 // 2], float(NT - 1), ALU.min))
                v(ts(halves(q1), PS[:, 0:2, 0:T2 // 2], float(NT * R), ALU.is_lt, None, ALU.add, accum_out=c0))
                v(cp(used[:, d:d + 1], c0))
                v(ts(halves(q1), PS[:, 0:2, 0:T2 // 2], float(NT * R - 1), ALU.min))
                v(stt(q1, q0, -float(R), q1, ALU.mult, ALU.add))
                v(cp(tile2[d], q0[64 * d:64 * d + 1, :]))
                v(cp(rel2[d], q1[64 * d + 32:64 * d + 33, :]))
                v(ts(pos, typ1, float(R), ALU.is_ge, FAR, ALU.mult))
                chains = ((t0, t1, pos), (t2, jf, sf))
                for there, before, to in chains:
                    v(dve.memset(before[:, 0:1], 0.0))
                v(dve.memset(sf, 0.0))
                v(dve.memset(shift[0:NT, R:R + 2], 0.0))

                def shifts(t, k):
                    v(ts(shiftb[0:NT, k % 4, :], onesf[0:NT, :], shift[0:NT, ds(t, 1)], ALU.mult))
                    dve.sem_inc(sort_in, 1)

                s_in = so.base
                for k in range(2):
                    shifts(k, k)
                with dve.Fori(0, R // 4) as i:
                    S.loop(i, 20)
                    for pair in range(2):
                        for k in range(2):
                            shifts(4 * i + 2 * pair + 2 + k, 2 * pair + 2 + k)
                        for k, (there, before, to) in enumerate(chains):
                            t = 4 * i + 2 * pair + k
                            dve.wait_ge(sort_out, s_in + t + 1)
                            lagged(dve.tensor_tensor_scan(before[:, 1:T1], onesw[:, 0:T1 - 1], PS[:, COLUMN_BANKS[2 * pair + k], 0:T1 - 1], 0.0,
                                                          ALU.mult, ALU.add))
                        for k, (there, before, to) in enumerate(chains):
                            lagged(tt(there, before, PS[:, PLACE_BANKS[2 * pair + k], 0:T1], ALU.add))
                        for k, (there, before, to) in enumerate(chains):
                            lagged(tt(there, there, masks[:, ds(4 * i + 2 * pair + k, 1), :].rearrange("p a j -> p (a j)"), ALU.mult))
                        for k, (there, before, to) in enumerate(chains):
                            lagged(tt(to, to, there, ALU.add))
                S.end(R // 4)
                so.base += R
                dve.wait_ge(vs, S.now)
                v(tt(pos, pos, sf, ALU.add))
                split(T1, pos)
                permute(T1, T2, AB1, dve.value_load(used[0:1, d:d + 1], min_val=1, max_val=T2))
                for h in range(0, T2, NARROW):
                    e = min(T2, h + NARROW)
                    v(ts(idx2[d][:, h:e], PS[:, 4 + h // NARROW, 0:e - h], float(OFF), ALU.add))
                    v(cp(q0[:, h:e].bitcast(i32), PS[:, 6 + h // NARROW, 0:e - h]))
                v(ts(q1.bitcast(i32), q0.bitcast(i32), 4, ALU.logical_shift_right))
                v(cp(lo2[d][:, 0:T2], q1.bitcast(i32)))
                if d == 0:
                    v(dve.memset(own_i, 4000))
                    v(dve.memset(oth_i, 0))
                    v(dve.memset(typ_i, 0))
                    dve.sem_inc(made, 1)
                    dve.wait_ge(product_out1, NT)
                    src_ = Hn[:, :, D:HW]
                    v(cp(stab[:, :, 0:H], src_))
                    v(tt(n0[:, :, :], src_, stab[:, :, 0:H], ALU.subtract))
                    v(cp(stab[:, :, H:2 * H], n0[:, :, :]))
                    v(tt(n0[:, :, :], n0[:, :, :], stab[:, :, H:2 * H], ALU.subtract))
                    v(cp(stab[:, :, 2 * H:3 * H], n0[:, :, :]))
                    dve.sem_inc(tab_ready, 1)
                    v(cp(M[:, :, :], src_))
                dve.sem_inc(sort_done, 1)

            v(dve.memset(asT, 0.0))
            dve.sem_inc(sort_done, 1)
            dve.sem_inc(max_taken, 2)

            def largest(n, u):
                dve.wait_ge(v_done, n + 3)
                dve.reduce_max(mx[:, u, :], PS[0:NL, (u % 2) * 2:(u % 2) * 2 + 2, :].rearrange("p b (h e) -> p (b h) e", h=4), AX.X).then_inc(max_taken, 1)

            def keep(n, u, tile):
                dve.wait_ge(max_taken, n + 3)
                dve.wait_ge(vs, S.now)
                m = M[:, ds(tile, 1), :].rearrange("p a h -> p (a h)")
                tt(m, m, mx[:, u, :], ALU.max).then_inc(vs, 1)
                S.step()

            def maxima(i, first=False):
                for u in range(8):
                    largest(8 * i + u, u)
                    if first and u == 0:
                        before = [None, *loads(dve, mybir.EngineType.DVE, tile1[0:1, 0:G], NT - 1)[0:G - 1]]
                    elif u % G == 0:
                        before = loads(dve, mybir.EngineType.DVE, tile1[0:1, ds(8 * i + u - 1, G)], NT - 1)
                    if u or not first:
                        keep(8 * i + u - 1, (u - 1) % 8, before[u % G])

            maxima(0, first=True)
            with dve.Fori(1, T1 // 8) as i:
                S.loop(i - 1, 8)
                maxima(i)
            S.end(T1 // 8 - 1)
            keep(T1 - 1, 7, loads(dve, mybir.EngineType.DVE, tile1[0:1, T1 - G:T1], NT - 1)[G - 1])
            dve.wait_ge(vs, S.now)

            a_src, a_dst = Hn[:, :, D:HW], Hn[:, :, HW:XW]
            v(tt(n0[:, :, :], M[:, :, :], a_dst, ALU.add))
            v(stt(ADC[:, :, H:2 * H], n0[:, :, :], 0.2, n0[:, :, :], ALU.mult, ALU.max))
            v(cp(ADC[:, :, 0:H], a_dst))
            v(tt(n0[:, :, :], a_src, a_dst, ALU.add))
            v(stt(n0[:, :, :], n0[:, :, :], 0.2, n0[:, :, :], ALU.mult, ALU.max))
            v(tt(n0[:, :, :], n0[:, :, :], ADC[:, :, H:2 * H], ALU.subtract))
            dve.sem_inc(shift_ready, 1)
            dve.wait_ge(self_exp, 1)

            def by_head(to, x, factors):
                def step(t):
                    heads = lambda y: y[:, ds(t, 1), 0:D].rearrange("p a (h c) -> p (a h) c", h=H)
                    return tt(heads(to), heads(x), factors[:, ds(t, 1), :].rearrange("p a (h o) -> p (a h) o", o=1).broadcast_to([NL, H, HC]), ALU.mult)
                every_tile(step)

            by_head(ACC[0], Hn, n1)
            v(cp(ACC[0][:, :, D:HW], n1[:, :, :]))

            dve.sem_inc(acc_taken, G)
            dve.sem_inc(hp_ready, 4 * G)

            def onehot(g, q, u):
                ts(oh[:, (G * q + u) % (4 * G), :], iota16[:, 1:NL + 1], lo1[:, ds(G * g + u, 1)], ALU.is_equal).then_inc(oh_ready, 1)

            def add_sum(g, u, tile):
                n = G * g + u
                dve.wait_ge(agg_done, n + 2 * G + 1)
                dve.wait_ge(acc_taken, n + G)
                m = ACC[0][:, ds(tile, 1), :].rearrange("p a f -> p (a f)")
                tt(m, m, PS[0:NL, 4 + u, 0:HW], ALU.add).then_inc(acc_taken, 1)

            def z_step(i, q, k):
                g = 4 * i + q
                q %= 4
                adc = PS[:, 2 + q % 2, 0:2 * H * G].rearrange("p (u k) -> p u k", u=G)
                z = [small[:, m, :].rearrange("p (u h) -> p u h", u=G) for m in range(3)]
                if k == 0:
                    dve.wait_ge(adc_done, G * g + 2 * G)
                    for u in range(G * q, G * q + G):
                        dve.wait_ge(gath_h[u], 16 * (i + 1))
                    tt(z[0], ring[:, G * q:G * q + G, D:HW], adc[:, :, 0:H], ALU.add).then_inc(vs, 1)
                elif k == 1:
                    stt(z[1], z[0], 0.2, z[0], ALU.mult, ALU.max).then_inc(vs, 1)
                else:
                    tt(z[2], z[1], adc[:, :, H:2 * H], ALU.subtract).then_inc(z_ready, 1)

            def attend(i, q, first=False, last=False, ahead=True):
                g = 4 * i + q
                tiles = None if first else loads(dve, mybir.EngineType.DVE, tile1[0:1, ds(G * g - G, G)], NT - 1)
                dve.wait_ge(p_ready, g + 1)
                for u in range(G):
                    if not first:
                        add_sum(g - 1, u, tiles[u])
                    rows, to = ring[:, G * q + u, :], scaled[:, G * (q % 2) + u, :]
                    tt(to[:, 0:D].rearrange("p (h c) -> p h c", h=H), rows[:, 0:D].rearrange("p (h c) -> p h c", h=H),
                       to[:, D:HW].rearrange("p (h o) -> p h o", o=1).broadcast_to([P, H, HC]), ALU.mult).then_inc(hp_ready, 1)
                    if u and not last:
                        if u > 1:
                            dve.wait_ge(vs, S.step())
                        z_step(i + (q + 1) // 4, (q + 1) % 4, u - 1)
                if ahead:
                    for u in range(G):
                        onehot(g + 3, q + 3, u)

            for q in range(3):
                for u in range(G):
                    onehot(q, q, u)
            for k in range(3):
                if k:
                    dve.wait_ge(vs, S.step())
                z_step(0, 0, k)
            for q in range(4):
                attend(0, q, first=q == 0)
            with dve.Fori(1, ROUNDS) as i:
                S.loop(i - 1, 8)
                for q in range(4):
                    attend(i, q)
            S.end(ROUNDS - 1)
            for q in range(TAIL):
                attend(ROUNDS, q, last=q == TAIL - 1, ahead=False)
            for u, tile in enumerate(loads(dve, mybir.EngineType.DVE, tile1[0:1, T1 - G:T1], NT - 1)):
                add_sum(T1 // G - 1, u, tile)
            dve.wait_ge(acc_taken, T1 + G)

            def layer_norm(to, k):
                def rows(x, t):
                    return x[:, ds(t, 1), 0:D].rearrange("p a f -> p (a f)")

                halves_ = n0[:, :, 0:6]
                every_tile(lambda t: dve.bn_stats(out=n0[:, ds(t, 1), 0:6].rearrange("p a s -> p (a s)"), in_=rows(ACC[0], t)))
                mean, apart, square = stat[:, :, 0:1], stat[:, :, 1:2], stat[:, :, 2:3]
                v(tt(mean, halves_[:, :, 1:2], halves_[:, :, 4:5], ALU.add))
                v(ts(mean, mean, 0.5, ALU.mult))
                v(tt(apart, halves_[:, :, 1:2], mean, ALU.subtract))
                v(tt(apart, apart, apart, ALU.mult))
                v(tt(square, halves_[:, :, 2:3], halves_[:, :, 5:6], ALU.add))
                v(stt(square, square, 1.0 / D, apart, ALU.mult, ALU.add))
                v(ts(square, square, LN_EPS, ALU.add))
                dve.sem_inc(ln_in, 1)
                dve.wait_ge(ln_act, k)
                v(dve.reciprocal(stat[:, :, 1], stat[:, :, 3]))
                every_tile(lambda t: ts(rows(to, t), rows(ACC[0], t), stat[:, ds(t, 1), 0:1].rearrange("p a o -> p (a o)"), ALU.subtract,
                                        stat[:, ds(t, 1), 1:2].rearrange("p a o -> p (a o)"), ALU.mult))

            def vec(k):
                return bc[0:NL, k - 2:k - 1, :].broadcast_to([NL, NT, D])

            o, j = ACC[0][:, :, 0:D], ACC[1][:, :, 0:D]
            v(ts(n0[:, :, :], ACC[0][:, :, D:HW], 1e-16, ALU.add))
            v(dve.reciprocal(n1[:, :, :], n0[:, :, :]))
            by_head(ACC[0], ACC[0], n1)
            v(tt(o, o, vec(2), ALU.add))
            layer_norm(ACC[0], 1)
            v(tt(o, o, vec(3), ALU.mult))
            v(tt(o, o, vec(4), ALU.add))
            v(tt(o, o, X[:, :, :], ALU.add))
            layer_norm(X, 2)
            v(cp(parts[:, :, 0:D], X[:, :, :]))
            v(tt(o, X[:, :, :], parts[:, :, 0:D], ALU.subtract))
            v(cp(parts[:, :, D:2 * D], o))
            v(tt(o, o, parts[:, :, D:2 * D], ALU.subtract))
            v(cp(low, o))
            dve.sem_inc(tab_ready, 1)

            v(dve.memset(ACC[0][:, :, 0:D + 1], 0.0))
            dve.wait_ge(x_out, 32)
            v(dve.memset(ACC[1][:, :, 0:D + 1], 0.0))
            for d in (0, 1):
                if d:
                    dve.wait_ge(over[0], 3)
                dve.sem_inc(y_taken[d], G)

                def onehot2(n, u):
                    ts(ohb[:, u, :], iota16[:, 1:NL + 1], lo2[d][:, ds(n, 1)], ALU.is_equal).then_inc(roh_ready[d], 1)

                for u in range(8):
                    onehot2(u, u)
                limit = dve.value_load(used[0:1, d:d + 1], min_val=1, max_val=T2)
                with dve.Fori(0, T2 // 8 // BLOCK) as block_:
                    with dve.If(block_ * (8 * BLOCK) < limit):
                        with dve.Fori(0, BLOCK) as j_:
                            i = block_ * BLOCK + j_
                            with dve.If(i * 8 < limit):
                                for g in range(2):
                                    tiles = loads(dve, mybir.EngineType.DVE, tile2[d][0:1, ds(8 * i + G * g, G)], NT - 1)
                                    for u in range(G):
                                        n = 8 * i + G * g + u
                                        dve.wait_ge(y_done[d], n + 8 + 1)
                                        dve.wait_ge(y_taken[d], n + G)
                                        m = ACC[d][:, ds(tiles[u], 1), 0:D + 1].rearrange("p a f -> p (a f)")
                                        tt(m, m, PS[0:NL, 4 + u, 0:D + 1], ALU.add).then_inc(y_taken[d], 1)
                                        onehot2(n + 8, G * g + u)
                dve.drain().then_inc(over[d], 1)
            dve.wait_ge(over[1], 3)

            for d in (0, 1):
                deg = ACC[d][:, :, D:D + 1]
                v(ts(stat[:, :, 0:1], deg, 1.0, ALU.max))
                v(dve.reciprocal(stat[:, :, 1:2], stat[:, :, 0:1]))
                v(ts(stat[:, :, 2:3], deg, 1.0, ALU.min))
                v(tt(ACC[d][:, :, 0:D], ACC[d][:, :, 0:D], stat[:, :, 1:2].broadcast_to([NL, NT, D]), ALU.mult))

                def bias(t):
                    m = ACC[d][:, ds(t, 1), 0:D].rearrange("p a f -> p (a f)")
                    return stt(m, bc[0:NL, 3 + d, :], stat[:, ds(t, 1), 2:3].rearrange("p a o -> p (a o)"), m, ALU.mult, ALU.add)
                every_tile(bias)
            v(tt(o, o, j, ALU.add))
            v(tt(o, o, vec(7), ALU.add))
            v(tt(o, o, X[:, :, :], ALU.add))
            dve.wait_ge(product_out2, NT)
            v(tt(o, o, looped, ALU.add))
            layer_norm(ACC[0], 3)
            dve.sem_inc(out_ready, 1)


NAMES = ("x", "src", "dst", "edge_type_16", "L0_gnn_W", "L0_gnn_att_src", "L0_gnn_att_dst", "L0_gnn_bias", "L0_gnn_ln_gamma",
         "L0_gnn_ln_beta", "L1_gnn_Wf", "L1_gnn_Wb", "L1_gnn_loop_weight", "L1_gnn_forward_bias", "L1_gnn_backward_bias",
         "L1_gnn_self_bias")


def kernel(**inputs):
    import concourse.bacc as bacc
    from concourse.bass_utils import run_bass_kernel_spmd

    nc = bacc.Bacc("TRN2", target_bir_lowering=False, num_devices=1)
    arrays, aps = {}, {}
    for name in NAMES:
        arrays[name] = np.ascontiguousarray(inputs[name])
        aps[name] = nc.dram_tensor(name, arrays[name].shape, mybir.dt.from_np(arrays[name].dtype), kind="ExternalInput").ap()
    out = nc.dram_tensor("result", (N, D), f32, kind="ExternalOutput").ap()
    build_program(nc, aps, out)
    ran = run_bass_kernel_spmd(nc, [arrays], core_ids=[0])
    return ran.results[0]["result"]
```
